# Optimizing a Trainium2 kernel written in Bass

```python
import numpy as np
import jax
import jax.numpy as jnp

def _softmax(x, axis=-1):
    return jax.nn.softmax(x, axis=axis)

def _gelu(x):
    return jax.nn.gelu(x, approximate=True)

def _silu(x):
    return jax.nn.silu(x)

def _sigmoid(x):
    return jax.nn.sigmoid(x)

def _layernorm(x, axis=-1, eps=1e-05):
    m = jnp.mean(x, axis=axis, keepdims=True)
    v = jnp.var(x, axis=axis, keepdims=True)
    return (x - m) / jnp.sqrt(v + eps)

def _scatter_add(tgt, idx, src, axis=0):
    return tgt.at[idx].add(src)

def _segment_sum(src, seg, n):
    return jax.ops.segment_sum(src, seg, n)
kernel_name = 'mk_xattn_ffn_d1_seqx_r4_634ee4'

def setup_inputs(seed: int=0):
    np.random.seed(seed)
    _w = jnp.asarray

    def _rec_inputs():
        import jax
        import jax.numpy as jnp
        _rk = jax.random.key(seed)
        x = -0.0003929 + 0.9999 * jax.random.normal(jax.random.fold_in(_rk, 1), (16, 128, 1024), jnp.float32)
        _lenS = 128 - jax.random.randint(jax.random.fold_in(_rk, 7), (16,), 0, max(1, 128 // 4) + 1, jnp.int32)
        _lenS2 = 128 - jax.random.randint(jax.random.fold_in(_rk, 8), (16,), 0, max(1, 128 // 4) + 1, jnp.int32)
        _ctx_4096P = jax.random.normal(jax.random.fold_in(_rk, 11), (16, 16, 1024), jnp.float32)
        _ctx_4096c = jax.random.dirichlet(jax.random.fold_in(_rk, 511), 0.3 * jnp.ones((16,), jnp.float32), (16, 128))
        _ctx_4096t = jnp.einsum('bsk,bkd->bsd', _ctx_4096c, _ctx_4096P)
        _ctx_4096t = _ctx_4096t * jax.lax.rsqrt(jnp.mean(jnp.square(_ctx_4096t)) + 1e-12) * 0.953939
        ctx_4096 = 2.81802e-05 + 1.00001 * (_ctx_4096t + 0.3 * jax.random.normal(jax.random.fold_in(_rk, 611), (16, 128, 1024), jnp.float32))
        return (x, ctx_4096)
    x, ctx_4096 = _rec_inputs()

    def _L0_xattn_setup():
        import jax, jax.numpy as jnp
        import numpy as np
        B, N, NKV = (2, 512, 512)
        E = 1024
        H = 16
        HD = E // H
        LQ = E // 8
        LKV = E // 16
        key = jax.random.key(seed)
        ks = jax.random.split(key, 6)
        Q = jax.random.normal(ks[0], (B, N, E), dtype=jnp.float32)
        K = jax.random.normal(ks[1], (B, NKV, E), dtype=jnp.float32)
        Wq_d = jax.random.normal(ks[2], (E, LQ), dtype=jnp.float32) / np.sqrt(E)
        W_qk = jax.random.normal(ks[3], (LQ, H * LKV), dtype=jnp.float32) / np.sqrt(LQ)
        Wkv_d = jax.random.normal(ks[4], (E, LKV), dtype=jnp.float32) / np.sqrt(E)
        Wv_u = jax.random.normal(ks[5], (LKV, H * HD), dtype=jnp.float32) / np.sqrt(LKV)
        return {'Q': Q, 'K': K, 'Wq_d': Wq_d, 'W_qk': W_qk, 'Wkv_d': Wkv_d, 'Wv_u': Wv_u}
    _L0_xattn_all = _L0_xattn_setup()
    _L0_xattn_in = {k: v for k, v in _L0_xattn_all.items() if k in ('Wq_d', 'W_qk', 'Wkv_d', 'Wv_u')}
    del _L0_xattn_all

    def _L0_ffn_setup():
        import jax, jax.numpy as jnp
        import numpy as np
        R = 16
        LORA_ALPHA = 16
        SCALING = LORA_ALPHA / R
        key = jax.random.key(seed)
        kx, kr, ka = jax.random.split(key, 3)
        B, S, D, DO, E = (4, 512, 1024, 1024, 8)
        x = jax.random.normal(kx, (B, S, D), dtype=jnp.float32)
        bound_r = 1.0 / np.sqrt(D)
        route_w = jax.random.uniform(kr, (E, D), jnp.float32, -bound_r, bound_r)
        bound_a = 1.0 / np.sqrt(D)
        A = jax.random.uniform(ka, (E, R, D), jnp.float32, -bound_a, bound_a)
        kb = jax.random.fold_in(key, 7)
        Bw = jax.random.normal(kb, (E, DO, R), dtype=jnp.float32) * 0.02
        return {'x': x, 'route_w': route_w, 'A': A, 'Bw': Bw}
    _L0_ffn_all = _L0_ffn_setup()
    _L0_ffn_in = {k: v for k, v in _L0_ffn_all.items() if k in ('route_w', 'A', 'Bw')}
    del _L0_ffn_all
    return {'x': x, 'ctx_4096': ctx_4096, 'L0_xattn_Wq_d': _L0_xattn_in['Wq_d'], 'L0_xattn_W_qk': _L0_xattn_in['W_qk'], 'L0_xattn_Wkv_d': _L0_xattn_in['Wkv_d'], 'L0_xattn_Wv_u': _L0_xattn_in['Wv_u'], 'L0_ffn_route_w': _L0_ffn_in['route_w'], 'L0_ffn_A': _L0_ffn_in['A'], 'L0_ffn_Bw': _L0_ffn_in['Bw']}

def reference(x, ctx_4096, L0_xattn_Wq_d, L0_xattn_W_qk, L0_xattn_Wkv_d, L0_xattn_Wv_u, L0_ffn_route_w, L0_ffn_A, L0_ffn_Bw):
    import jax
    import jax.numpy as jnp

    def _L0_xattn_ref(Q, K, Wq_d, W_qk, Wkv_d, Wv_u):
        import jax, jax.numpy as jnp
        import numpy as np
        B, N, NKV = (2, 512, 512)
        E = 1024
        H = 16
        HD = E // H
        LQ = E // 8
        LKV = E // 16
        b, n, _ = Q.shape
        nkv = K.shape[1]
        C_q = Q @ Wq_d
        C_kv = K @ Wkv_d
        CqWqk = (C_q @ W_qk).reshape(b, n, H, LKV)
        scores = jnp.einsum('bnhl,bkl->bhnk', CqWqk, C_kv) / jnp.sqrt(jnp.asarray(LKV, dtype=Q.dtype))
        attn = jax.nn.softmax(scores, axis=-1)
        V_up = (C_kv @ Wv_u).reshape(b, nkv, H, HD)
        out = jnp.einsum('bhnk,bkhd->bnhd', attn, V_up)
        return out.reshape(b, n, H * HD)

    def _L0_ffn_ref(x, route_w, A, Bw):
        import jax, jax.numpy as jnp
        import numpy as np
        R = 16
        LORA_ALPHA = 16
        SCALING = LORA_ALPHA / R
        logits = jnp.einsum('bsd,ed->bse', x, route_w)
        topk_v, topk_idx = jax.lax.top_k(logits, 1)
        E = logits.shape[-1]
        route_weight = jax.nn.one_hot(topk_idx[..., 0], E, dtype=logits.dtype) * topk_v
        h = jnp.einsum('bsd,erd->bser', x, A)
        wh = route_weight[..., None] * h
        out = jnp.einsum('bser,eor->bso', wh, Bw) * SCALING
        return out
    x = x + _L0_xattn_ref(_layernorm(x, axis=-1), ctx_4096, L0_xattn_Wq_d, L0_xattn_W_qk, L0_xattn_Wkv_d, L0_xattn_Wv_u)
    x = x + _L0_ffn_ref(_layernorm(x, axis=-1), L0_ffn_route_w, L0_ffn_A, L0_ffn_Bw)
    return x

_drawn_inputs = setup_inputs


def setup_inputs(seed=0):
    import zlib

    import numpy as np

    out = dict(_drawn_inputs(seed))
    spreads = {}
    factors = {}
    for name, (base, spread) in spreads.items():
        noise = np.random.default_rng([zlib.crc32(name.encode()), seed]).standard_normal(out[name].shape)
        drawn = base * np.exp(spread * noise) if base else spread * noise
        out[name] = jnp.asarray(drawn.astype(out[name].dtype))
    for name, factor in factors.items():
        out[name] = (out[name] * factor).astype(out[name].dtype)
    return out
```

```python
import concourse.bass as bass
from concourse import mybir
from contextlib import ExitStack



def xattn_ffn_kernel(nc, x, ctx_in, w_q, w_qk, w_kv, w_v, route_w, a_w, b_w, out):
    f32, f16 = mybir.dt.float32, mybir.dt.float16
    ALU, ACT, AX = mybir.AluOpType, mybir.ActivationFunctionType, mybir.AxisListType

    NB, P, E = x.shape
    LQ = w_q.shape[1]
    L = w_kv.shape[1]
    H = w_qk.shape[1] // L
    HD = w_v.shape[1] // H
    NX, R, _ = a_w.shape
    ER = NX * R
    HR = ER + NX
    C = E // P
    HC = C // 2
    BANK = 512
    G4 = 4
    NG = H // G4
    OB = BANK // (HD + 1)
    OM = H - 2 * OB
    EPS = 1e-5
    WS = 16.0
    BS = 64.0
    MS = 64.0
    SOFT = 1.0 / (WS * L ** 0.5)
    FS = 1.0 / (WS * BS)
    RING = 4
    FIRST, LAST, LOOP = -1, NB + 1, (2, NB - 2)

    with ExitStack() as stack:
        def sb(name, shape, dt):
            return stack.enter_context(nc.sbuf_tensor(name, shape, dt))

        def pb(name, shape):
            return stack.enter_context(nc.psum_tensor(name, shape, f32))

        def sem(name):
            return stack.enter_context(nc.semaphore(name))

        wq = sb("wq", [P, C, LQ], f32)
        wkv2 = sb("wkv2", [P, C, 2, L], f32)
        wqk_f = sb("wqk_f", [P, C, 2, L], f32)
        wqk_hi = sb("wqk_hi", [P, C, 2 * L], f16)
        wqk_lo = sb("wqk_lo", [P, C, 2 * L], f16)
        wv_f = sb("wv_f", [P, E], f32)
        wv_hi = sb("wv_hi", [P, E], f16)
        wv_st = sb("wv_st", [P, E], f16)
        a_f = sb("a_f", [P, E], f32)
        r_f = sb("r_f", [NX, E], f32)
        ar = sb("ar", [P, C, HR], f32)
        b_f = sb("b_f", [P, C, NX, R], f32)
        b_hi = sb("b_hi", [P, E], f16)
        b_lo = sb("b_lo", [P, E], f16)
        ident = sb("ident", [P, P], f32)
        pick = sb("pick", [H, H, P], f16)
        prefer = sb("prefer", [P, NX], f32)
        mhalf = sb("mhalf", [P, 1], f32)
        x_sb = sb("x_sb", [P, RING, E], f32)
        c_sb = sb("c_sb", [P, RING, E], f32)
        xn = sb("xn", [P, 2, E], f32)
        xT = sb("xT", [P, C, P], f32)
        cT = sb("cT", [P, C, P], f32)
        q_hi = sb("q_hi", [P, P], f16)
        q_lo = sb("q_lo", [P, P], f16)
        k_hi = sb("k_hi", [P, 2, P], f16)
        k_lo = sb("k_lo", [P, 2, P], f16)
        g_hi = sb("g_hi", [P, 2, C, P], f16)
        g_lo = sb("g_lo", [P, 2, C, P], f16)
        v_sb = sb("v_sb", [P, 2, H, HD + 1], f32)
        nmax = sb("nmax", [P, H], f32)
        nmaxT = sb("nmaxT", [H, P], f16)
        prob = sb("prob", [P, NG, BANK], f32)
        rsum = sb("rsum", [P, H], f32)
        o_sb = sb("o_sb", [P, 2, E], f32)
        y_sb = sb("y_sb", [P, RING, E], f32)
        yn = sb("yn", [P, 2, E], f32)
        yT = sb("yT", [P, C, P], f32)
        h_sb = sb("h_sb", [P, HR], f32)
        top = sb("top", [P, 4], f32)
        tie = sb("tie", [P, NX], f32)
        rw = sb("rw", [P, NX], f32)
        wh = sb("wh", [P, NX, R], f32)
        w_hi = sb("w_hi", [P, P], f16)
        w_lo = sb("w_lo", [P, P], f16)
        o_out = sb("o_out", [P, 2, E], f32)
        bn = sb("bn", [P, 2, 2, 6], f32)
        mv = sb("mv", [P, 2, 2, 2], f32)
        ln = sb("ln", [P, 2, 3], f32)

        T = pb("T", [P, 2, BANK])
        S = pb("S", [P, BANK])
        D = pb("D", [P, 2, BANK])
        O = pb("O", [P, 2, BANK])
        M = pb("M", [P, BANK])

        x_in = [sem(f"x_in{n}") for n in range(RING)]
        c_in = [sem(f"c_in{n}") for n in range(RING)]
        wq_in, wkv_in, wqk_in, wv_in, a_in, b_in = (sem(n) for n in (
            "wq_in", "wkv_in", "wqk_in", "wv_in", "a_in", "b_in"))
        consts, apart = sem("consts"), sem("apart")
        wqk_ready, wvh_ready, wv_ready = sem("wqk_ready"), sem("wvh_ready"), sem("wv_ready")
        a_tr, a_ready, r_tr, r_ready = sem("a_tr"), sem("a_ready"), sem("r_tr"), sem("r_ready")
        b_tr, bhi_ready, b_ready = sem("b_tr"), sem("bhi_ready"), sem("b_ready")
        x_bn2, y_bn2, x_stat, y_stat = sem("x_bn2"), sem("y_bn2"), sem("x_stat"), sem("y_stat")
        x_ln, y_ln = sem("x_ln"), sem("y_ln")
        xn_ready, yn_ready, y_ready = sem("xn_ready"), sem("yn_ready"), sem("y_ready")
        xT_mm2, xT_ready2 = sem("xT_mm2"), sem("xT_ready2")
        cT_mm2, cT_ready2 = sem("cT_mm2"), sem("cT_ready2")
        yT_mm2, yT_ready2 = sem("yT_mm2"), sem("yT_ready2")
        q_mm, qhi_ready, qlo_ready = sem("q_mm"), sem("qhi_ready"), sem("qlo_ready")
        k_mm, khi_ready, klo_ready = sem("k_mm"), sem("khi_ready"), sem("klo_ready")
        g_mm2, ghi_ready2, glo_ready2 = sem("g_mm2"), sem("ghi_ready2"), sem("glo_ready2")
        v_mm2, v_ready2 = sem("v_mm2"), sem("v_ready2")
        s_mm4, max_ready4 = sem("s_mm4"), sem("max_ready4")
        nT_mm, nT_ready = sem("nT_mm"), sem("nT_ready")
        d_mm4, exp_ready4 = sem("d_mm4"), sem("exp_ready4")
        pv_mm4, om_ready, o_ready = sem("pv_mm4"), sem("om_ready"), sem("o_ready")
        h_mm, h_ready, wh_ready = sem("h_mm"), sem("h_ready"), sem("wh_ready")
        wT_mm, whi_ready, wlo_ready = sem("wT_mm"), sem("whi_ready"), sem("wlo_ready")
        f_mm2, out_ready2 = sem("f_mm2"), sem("out_ready2")
        stored = [sem(f"stored{n}") for n in range(2)]
        o_step2, route4, pool_chain = sem("o_step2"), sem("route4"), sem("pool_chain")

        def live(b):
            return not isinstance(b, int) or 0 <= b < NB

        def at(i, n):
            return isinstance(i, int) and i == n

        def wait(eng, s, n):
            if not isinstance(n, int) or n > 0:
                eng.wait_ge(s, n)

        def wait_apart(eng, s, n):
            wait(eng, s, n)
            eng.sem_inc(apart, 1)

        def arrived(eng, s, b, m, ring):
            eng.wait_ge(s[m], (16 // ring) * (b - m) + 16)

        def pipeline(eng, iteration, first=FIRST, loop=LOOP, last=LAST):
            for i in range(first, loop[0]):
                iteration(i, i % RING)
            with eng.Fori(loop[0], loop[1] - RING + 1, RING) as i0:
                for n in range(RING):
                    iteration(i0 + n, (loop[0] + n) % RING)
            for i in range(loop[1], last + 1):
                iteration(i, i % RING)

        block = stack.enter_context(nc.Block())

        @block.sync
        def _(sp):
            def load(b, m):
                sp.dma_start(x_sb[:, m, :], x[b, :, :]).then_inc(x_in[m], 16)
                sp.dma_start(c_sb[:, m, :], ctx_in[b, :, :]).then_inc(c_in[m], 16)

            load(0, 0)
            sp.dma_start(wq[:], w_q.rearrange("(c p) n -> p c n", p=P)).then_inc(wq_in, 16)
            kv = w_kv.rearrange("(c p) n -> p c n", p=P)
            sp.dma_start(wkv2[:, :, 0, :], kv).then_inc(wkv_in, 16)
            sp.dma_start(wkv2[:, :, 1, :], kv).then_inc(wkv_in, 16)
            qk = w_qk.rearrange("p (t c l) -> p t c l", t=2, l=L)
            for t in range(2):
                sp.dma_start(wqk_f[:, :, t, :], qk[:, t, :, :]).then_inc(wqk_in, 16)
            for t in range(2):
                sp.dma_start(wv_f[t * L:(t + 1) * L, :], w_v).then_inc(wv_in, 16)
            load(1, 1)
            sp.dma_start(a_f[:], a_w.rearrange("e r d -> (e r) d")).then_inc(a_in, 16)
            sp.dma_start(r_f[:], route_w).then_inc(a_in, 16)
            load(2, 2)
            bw = b_w.rearrange("e (c p) r -> p c e r", p=P)
            for c in range(C):
                sp.dma_start(b_f[:, c, :, :], bw[:, c, :, :]).then_inc(b_in, 16)
            load(3, 3)

            def iteration(i, m):
                b = i + RING
                if live(b):
                    wait(sp, y_ready, i + 1)
                    sp.wait_ge(cT_mm2, 2 * i + 2)
                    load(b, m)
                b = i - 2
                if live(b):
                    sp.wait_ge(out_ready2, 2 * b + 2)
                    sp.dma_start(out[b, :, :], o_out[:, m % 2, :]).then_inc(stored[m % 2], 16)

            pipeline(sp, iteration, first=0, loop=(2, 10))
            for n in range(2):
                sp.wait_ge(stored[n], 16 * (NB // 2))

        @block.gpsimd
        def _(pool):
            chain = [0]

            def link(ins):
                chain[0] += 1
                ins.then_inc(pool_chain, 1)
                pool.wait_ge(pool_chain, chain[0])

            link(nc.gpsimd.memset(ident[:], 0.0))
            nc.gpsimd.affine_select(out=ident[:], in_=ident[:], compare_op=ALU.not_equal, fill=1.0, base=0,
                                    pattern=[[-1, P]], channel_multiplier=1).then_inc(consts, 1)
            link(nc.gpsimd.memset(mhalf[:], -0.5))
            link(nc.gpsimd.memset(pick[:], 0.0))
            nc.gpsimd.affine_select(out=pick[:], in_=pick[:], compare_op=ALU.not_equal, fill=MS, base=0,
                                    pattern=[[-1, H], [0, P]], channel_multiplier=1).then_inc(consts, 1)
            for e in range(NX):
                nc.gpsimd.memset(prefer[:, e:e + 1], float(NX - e)).then_inc(consts, 1)
            nc.gpsimd.memset(v_sb[:, :, :, HD:HD + 1], WS).then_inc(consts, 1)

            def normalise(dst, src, stat, which, b, ln_step, done):
                wait_apart(pool, done, b)
                part = ln[:, which, :]
                nc.gpsimd.tensor_scalar(part[:, 0:1], stat[:, 0:1], -1.0, 0.0, ALU.mult, ALU.add).then_inc(ln_step, 1)
                nc.gpsimd.tensor_scalar(part[:, 1:2], stat[:, 1:2], 1.0, EPS, ALU.mult, ALU.add).then_inc(ln_step, 1)
                wait_apart(pool, ln_step, 3 * b + 2)
                nc.gpsimd.tensor_tensor(part[:, 2:3], part[:, 1:2], mhalf[:], ALU.pow).then_inc(ln_step, 1)
                wait_apart(pool, ln_step, 3 * b + 3)
                nc.gpsimd.tensor_scalar(dst, src, part[:, 0:1], part[:, 2:3], ALU.add, ALU.mult).then_inc(done, 1)

            def iteration(i, m):
                b = i - 1
                if live(b):
                    pool.wait_ge(y_stat, b + 1)
                    wait(pool, yT_mm2, 2 * (b - 1))
                    normalise(yn[:, (m - 1) % 2, :], y_sb[:, (m - 1) % RING, :], mv[:, 1, (m - 1) % 2, :],
                              1, b, y_ln, yn_ready)
                b = i + 2
                if live(b):
                    pool.wait_ge(x_stat, b + 1)
                    wait(pool, xT_mm2, 2 * (b - 1))
                    normalise(xn[:, m % 2, :], x_sb[:, (m + 2) % RING, :], mv[:, 0, m % 2, :],
                              0, b, x_ln, xn_ready)
                b = i
                if live(b):
                    pool.wait_ge(o_ready, b + 1)
                    wait(pool, out_ready2, 2 * (b - 2))
                    nc.gpsimd.tensor_tensor(y_sb[:, m, :], x_sb[:, m, :], o_sb[:, m % 2, :],
                                            ALU.add).then_inc(y_ready, 1)

            pipeline(pool, iteration, first=FIRST - 1)

        @block.vector
        def _(dve):
            dve.wait_ge(wqk_in, 32)
            dve.wait_ge(wqk_ready, 1)
            nc.vector.scalar_tensor_tensor(wqk_lo[:], wqk_f[:].rearrange("p c t l -> p c (t l)"), WS, wqk_hi[:],
                                           ALU.mult, ALU.subtract).then_inc(wqk_ready, 1)
            dve.wait_ge(wv_in, 32)
            dve.wait_ge(wvh_ready, 1)
            nc.vector.scalar_tensor_tensor(wv_st[L:P, :], wv_f[L:P, :], WS, wv_hi[L:P, :],
                                           ALU.mult, ALU.subtract).then_inc(wv_ready, 1)

            def statistics(src, which, b, slot, step, done):
                wait(dve, done, b)
                for k in range(2):
                    nc.vector.bn_stats(bn[:, which, k, :], src[:, k * BANK:(k + 1) * BANK]).then_inc(step, 1)
                wait_apart(dve, step, 2 * b + 2)
                nc.vector.bn_aggr(mv[:, which, slot, :], bn[:, which, :, :]).then_inc(done, 1)

            def iteration(i, m):
                b = i - 1
                if live(b):
                    dve.wait_ge(y_ready, b + 1)
                    wait(dve, yn_ready, b - 1)
                    statistics(y_sb[:, (m - 1) % RING, :], 1, b, (m - 1) % 2, y_bn2, y_stat)
                b = i - 2
                if live(b):
                    dve.wait_ge(whi_ready, b + 1)
                    wait(dve, f_mm2, 2 * b)
                    nc.vector.scalar_tensor_tensor(w_lo[:], M[:, 0:P], WS, w_hi[:], ALU.mult,
                                                   ALU.subtract).then_inc(wlo_ready, 1)
                b = i + 1
                if live(b):
                    dve.wait_ge(qhi_ready, b + 1)
                    wait(dve, g_mm2, 2 * b)
                    nc.vector.tensor_tensor(q_lo[:], M[:, 0:P], q_hi[:], ALU.subtract).then_inc(qlo_ready, 1)
                b = i + 2
                if live(b):
                    arrived(dve, x_in, b, (m + 2) % RING, RING)
                    wait(dve, xn_ready, b - 1)
                    statistics(x_sb[:, (m + 2) % RING, :], 0, b, m % 2, x_bn2, x_stat)
                b, s = i + 1, (m + 1) % 2
                if live(b):
                    wait(dve, d_mm4, NG * (b - 1))
                    for k in range(2):
                        dve.wait_ge(ghi_ready2, 2 * b + k + 1)
                        nc.vector.tensor_tensor(g_lo[:, s, k * HC:(k + 1) * HC, :], T[:, k, :].rearrange(
                            "p (j t) -> p j t", t=P), g_hi[:, s, k * HC:(k + 1) * HC, :],
                            ALU.subtract).then_inc(glo_ready2, 1)
                    dve.wait_ge(khi_ready, b + 1)
                    nc.vector.tensor_tensor(k_lo[:, s, :], M[:, 0:P], k_hi[:, s, :],
                                            ALU.subtract).then_inc(klo_ready, 1)
                    wait(dve, nT_mm, b)
                for g in range(NG):
                    b = i + 1
                    if live(b):
                        dve.wait_ge(s_mm4, NG * b + g + 1)
                        h0 = C * (g % 2) + G4 * (g // 2)
                        nc.vector.tensor_reduce(nmax[:, h0:h0 + G4], S[:].rearrange("p (h t) -> p h t", t=P),
                                                AX.X, ALU.max, negate=True).then_inc(max_ready4, 1)
                    b = i
                    if g == 0 and live(b):
                        dve.wait_ge(pv_mm4, NG * b + NG)
                        wait(dve, y_ready, b - 1)
                        om = M[:, 0:OM * (HD + 1)].rearrange("p (h d) -> p h d", h=OM)
                        oe = O[:, :, 0:OB * (HD + 1)].rearrange("p k (h d) -> p k h d", h=OB)
                        slot = o_sb[:, m % 2, :]
                        nc.vector.reciprocal(rsum[:, 2 * OB:H], om[:, :, HD]).then_inc(o_step2, 1)
                        dve.wait_ge(o_step2, 2 * b + 1)
                        nc.vector.tensor_tensor(
                            slot[:, 2 * OB * HD:E].rearrange("p (h d) -> p h d", h=OM), om[:, :, 0:HD],
                            rsum[:, 2 * OB:H].unsqueeze(2).broadcast_to([P, OM, HD]), ALU.mult).then_inc(om_ready, 1)
                        re = rsum[:, 0:2 * OB].rearrange("p (k h) -> p k h", k=2)
                        nc.vector.reciprocal(re, oe[:, :, :, HD]).then_inc(o_step2, 1)
                        dve.wait_ge(o_step2, 2 * b + 2)
                        nc.vector.tensor_tensor(
                            slot[:, 0:2 * OB * HD].rearrange("p (k h d) -> p k h d", k=2, h=OB), oe[:, :, :, 0:HD],
                            re.unsqueeze(3).broadcast_to([P, 2, OB, HD]), ALU.mult).then_inc(o_ready, 1)
                b = i - 1
                if live(b):
                    dve.wait_ge(h_ready, b + 1)
                    wait(dve, wT_mm, b)
                    logits = h_sb[:, ER:HR]
                    nc.vector.tensor_reduce(top[:, 0:1], logits, AX.X, ALU.max).then_inc(route4, 1)
                    dve.wait_ge(route4, 4 * b + 1)
                    nc.vector.scalar_tensor_tensor(tie[:], logits, top[:, 0:1], prefer[:], ALU.is_equal,
                                                   ALU.mult).then_inc(route4, 1)
                    dve.wait_ge(route4, 4 * b + 2)
                    nc.vector.tensor_reduce(top[:, 1:2], tie[:], AX.X, ALU.max).then_inc(route4, 1)
                    dve.wait_ge(route4, 4 * b + 3)
                    nc.vector.tensor_scalar(rw[:], tie[:], top[:, 1:2], top[:, 0:1], ALU.is_equal,
                                            ALU.mult).then_inc(route4, 1)
                    dve.wait_ge(route4, 4 * b + 4)
                    nc.vector.tensor_tensor(wh[:], h_sb[:, 0:ER].rearrange("p (e r) -> p e r", e=NX),
                                            rw[:].unsqueeze(2).broadcast_to([P, NX, R]),
                                            ALU.mult).then_inc(wh_ready, 1)
                b = i - 2
                if live(b):
                    wait(dve, stored[m % 2], 8 * (b - m % 2))
                    for k in range(2):
                        dve.wait_ge(f_mm2, 2 * b + k + 1)
                        half = slice(k * BANK, (k + 1) * BANK)
                        nc.vector.scalar_tensor_tensor(o_out[:, m % 2, half], T[:, k, :], FS,
                                                       y_sb[:, (m - 2) % RING, half], ALU.mult,
                                                       ALU.add).then_inc(out_ready2, 1)
                if at(i, FIRST):
                    for k in range(2):
                        dve.wait_ge(bhi_ready, k + 1)
                        half = slice(k * BANK, (k + 1) * BANK)
                        nc.vector.scalar_tensor_tensor(b_lo[:, half], T[:, k, :], BS, b_hi[:, half], ALU.mult,
                                                       ALU.subtract).then_inc(b_ready, 1)

            dve.wait_ge(consts, 1 + 1 + NX + 1)
            pipeline(dve, iteration, first=FIRST - 1)

        @block.scalar
        def _(act):
            act.wait_ge(wqk_in, 32)
            nc.scalar.activation(wqk_hi[:], wqk_f[:].rearrange("p c t l -> p c (t l)"), ACT.Copy,
                                 scale=WS).then_inc(wqk_ready, 1)
            act.wait_ge(wv_in, 32)
            nc.scalar.activation(wv_hi[L:P, :], wv_f[L:P, :], ACT.Copy, scale=WS).then_inc(wvh_ready, 1)
            nc.scalar.activation(wv_st[0:L, :], wv_f[0:L, :], ACT.Copy, scale=WS).then_inc(wv_ready, 1)

            def copy_out(dst, mm, free, free_n, done, b):
                wait(act, free, free_n)
                for k in range(2):
                    act.wait_ge(mm, 2 * b + k + 1)
                    nc.scalar.activation(dst[:, k * HC:(k + 1) * HC, :], T[:, k, :].rearrange(
                        "p (j t) -> p j t", t=P), ACT.Copy).then_inc(done, 1)

            def exps(b, g):
                act.wait_ge(d_mm4, NG * b + g + 1)
                wait(act, pv_mm4, NG * (b - 1) + g + 1)
                nc.scalar.activation(prob[:, g, :], D[:, g % 2, :], ACT.Exp, scale=SOFT).then_inc(exp_ready4, 1)

            def iteration(i, m):
                s = (m + 1) % 2
                if live(i + 1):
                    copy_out(xT, xT_mm2, q_mm, i + 1, xT_ready2, i + 1)
                b = i - 2
                if live(b):
                    act.wait_ge(wT_mm, b + 1)
                    wait(act, f_mm2, 2 * b)
                    nc.scalar.activation(w_hi[:], M[:, 0:P], ACT.Copy, scale=WS).then_inc(whi_ready, 1)
                if live(i):
                    exps(i, 1)
                b = i + 1
                if live(b):
                    copy_out(cT, cT_mm2, k_mm, b, cT_ready2, b)
                    act.wait_ge(q_mm, b + 1)
                    wait(act, g_mm2, 2 * b)
                    nc.scalar.activation(q_hi[:], M[:, 0:P], ACT.Copy).then_inc(qhi_ready, 1)
                if live(i):
                    exps(i, 2)
                if live(b):
                    wait(act, d_mm4, NG * (b - 1))
                    wait(act, v_mm2, 2 * (b - 1))
                    for k in range(2):
                        act.wait_ge(g_mm2, 2 * b + k + 1)
                        nc.scalar.activation(g_hi[:, s, k * HC:(k + 1) * HC, :], T[:, k, :].rearrange(
                            "p (j t) -> p j t", t=P), ACT.Copy).then_inc(ghi_ready2, 1)
                    act.wait_ge(k_mm, b + 1)
                    nc.scalar.activation(k_hi[:, s, :], M[:, 0:P], ACT.Copy).then_inc(khi_ready, 1)
                if live(i - 1):
                    copy_out(yT, yT_mm2, h_mm, i - 1, yT_ready2, i - 1)
                if live(i):
                    exps(i, 3)
                if live(b):
                    wait(act, pv_mm4, NG * (b - 1))
                    for k in range(2):
                        act.wait_ge(v_mm2, 2 * b + k + 1)
                        nc.scalar.activation(v_sb[:, s, k * (H // 2):(k + 1) * (H // 2), 0:HD], T[:, k, :].rearrange(
                            "p (h d) -> p h d", d=HD), ACT.Copy).then_inc(v_ready2, 1)
                if live(i - 1):
                    act.wait_ge(h_mm, i)
                    wait(act, wh_ready, i - 1)
                    nc.scalar.activation(h_sb[:], M[:, 0:HR], ACT.Copy).then_inc(h_ready, 1)
                if live(b):
                    act.wait_ge(nT_mm, b + 1)
                    wait(act, d_mm4, NG * b)
                    nc.scalar.activation(nmaxT[:], M[0:H, 0:P], ACT.Copy, scale=1.0 / MS).then_inc(nT_ready, 1)
                if at(i, FIRST):
                    for k in range(2):
                        act.wait_ge(a_tr, k + 1)
                        nc.scalar.activation(ar[:, k * HC:(k + 1) * HC, 0:ER], T[:, k, :].rearrange(
                            "p (j t) -> p j t", t=P), ACT.Copy).then_inc(a_ready, 1)
                    act.wait_ge(r_tr, 1)
                    nc.scalar.activation(ar[:, :, ER:HR], M[:, 0:C * NX].rearrange("p (c e) -> p c e", e=NX),
                                         ACT.Copy).then_inc(r_ready, 1)
                    for k in range(2):
                        act.wait_ge(b_tr, k + 1)
                        nc.scalar.activation(b_hi[:, k * BANK:(k + 1) * BANK], T[:, k, :], ACT.Copy,
                                             scale=BS).then_inc(bhi_ready, 1)
                if live(b):
                    exps(b, 0)

            pipeline(act, iteration)

        @block.tensor
        def _(pe):
            def transposes(src, mm):
                for c in range(C):
                    last = nc.tensor.transpose(T[:, c // HC, (c % HC) * P:(c % HC + 1) * P],
                                               src[:, c * P:(c + 1) * P], ident[:])
                    if c % HC == HC - 1:
                        last.then_inc(mm, 1)

            def scores(b, m, g):
                pe.wait_ge(khi_ready, b + 1) if g == 0 else None
                if g == 0:
                    pe.wait_ge(klo_ready, b + 1)
                    pe.wait_ge(glo_ready2, 2 * b + 2)
                    pe.wait_ge(nT_ready, b + 1)
                wait(pe, exp_ready4, NG * b + g - 1)
                s, j0 = m % 2, G4 * (g // 2)
                rows = slice(L * (g % 2), L * (g % 2 + 1))
                d = D[:, g % 2, :]
                hi = g_hi[rows, s, j0:j0 + G4, :].rearrange("p j t -> p (j t)")
                lo = g_lo[rows, s, j0:j0 + G4, :].rearrange("p j t -> p (j t)")
                nc.tensor.matmul(d, k_hi[rows, s, :], hi, start=True, stop=False)
                nc.tensor.matmul(d, k_hi[rows, s, :], lo, start=False, stop=False)
                nc.tensor.matmul(d, k_lo[rows, s, :], hi, start=False, stop=False)
                for n in range(G4):
                    last = nc.tensor.matmul(d[:, n * P:(n + 1) * P], pick[:, C * (g % 2) + j0 + n, :], nmaxT[:],
                                            start=False, stop=(n == G4 - 1))
                last.then_inc(d_mm4, 1)

            def outputs(b, m, g):
                if g == 0:
                    pe.wait_ge(v_ready2, 2 * b + 2)
                    wait(pe, o_ready, b)
                pe.wait_ge(exp_ready4, NG * b + g + 1)
                for n in range(G4):
                    h = C * (g % 2) + G4 * (g // 2) + n
                    bank = M if h >= 2 * OB else O[:, h // OB, :]
                    col = (h % OB) * (HD + 1)
                    last = nc.tensor.matmul(bank[:, col:col + HD + 1], prob[:, g, n * P:(n + 1) * P],
                                            v_sb[:, m % 2, h, :], start=True, stop=True)
                last.then_inc(pv_mm4, 1)

            def maxima(b, m, g):
                if g == 0:
                    pe.wait_ge(khi_ready, b + 1)
                    pe.wait_ge(ghi_ready2, 2 * b + 2)
                wait(pe, max_ready4, NG * b + g)
                rows = slice(L * (g % 2), L * (g % 2 + 1))
                for n in range(G4):
                    last = nc.tensor.matmul(S[:, n * P:(n + 1) * P], g_hi[rows, m % 2, G4 * (g // 2) + n, :],
                                            k_hi[rows, m % 2, :], start=True, stop=True)
                last.then_inc(s_mm4, 1)

            def experts(b, k):
                pe.wait_ge(yT_ready2, 2 * b + k + 1)
                for c in range(k * HC, (k + 1) * HC):
                    last = nc.tensor.matmul(M[:, 0:HR], yT[:, c, :], ar[:, c, :], start=(c == 0), stop=(c == C - 1))
                if k == 1:
                    last.then_inc(h_mm, 1)

            def iteration(i, m):
                n1, n1s = i + 1, (m + 1) % 2
                if live(n1):
                    pe.wait_ge(xn_ready, n1 + 1)
                    wait(pe, v_ready2, 2 * n1)
                    if not isinstance(i, int) or i >= 3:
                        pe.wait_ge(out_ready2, 2 * (i - 3) + 2)
                    transposes(xn[:, n1s, :], xT_mm2)
                b = i - 2
                if live(b):
                    pe.wait_ge(wh_ready, b + 1)
                    wait(pe, nT_ready, min(b + 3, NB) if isinstance(b, int) else b + 3)
                    nc.tensor.transpose(M[:, 0:P], wh[:].rearrange("p e r -> p (e r)"), ident[:]).then_inc(wT_mm, 1)
                if live(i):
                    outputs(i, m, 0)
                    scores(i, m, 1)
                if live(n1):
                    arrived(pe, c_in, n1, (m + 1) % RING, RING)
                    pe.wait_ge(xT_ready2, 2 * n1 + 2)
                    transposes(c_sb[:, (m + 1) % RING, :], cT_mm2)
                    if live(i - 2):
                        pe.wait_ge(wlo_ready, i - 1)
                    else:
                        wait(pe, nT_ready, n1)
                    for c in range(C):
                        last = nc.tensor.matmul(M[:, 0:P], wq[:, c, :], xT[:, c, :], start=(c == 0), stop=(c == C - 1))
                    last.then_inc(q_mm, 1)
                if live(i):
                    outputs(i, m, 1)
                    scores(i, m, 2)
                if live(n1):
                    pe.wait_ge(cT_ready2, 2 * n1 + 2)
                    pe.wait_ge(qlo_ready, n1 + 1)
                    for j in range(C):
                        g = T[:, j // HC, (j % HC) * P:(j % HC + 1) * P]
                        nc.tensor.matmul(g, wqk_hi[:, j, :], q_hi[:], start=True, stop=False)
                        nc.tensor.matmul(g, wqk_hi[:, j, :], q_lo[:], start=False, stop=False)
                        last = nc.tensor.matmul(g, wqk_lo[:, j, :], q_hi[:], start=False, stop=True)
                        if j % HC == HC - 1:
                            last.then_inc(g_mm2, 1)
                    for c in range(C):
                        last = nc.tensor.matmul(M[:, 0:P], wkv2[:, c, :, :].rearrange("p t l -> p (t l)"),
                                                cT[:, c, :], start=(c == 0), stop=(c == C - 1))
                    last.then_inc(k_mm, 1)
                if live(i - 1):
                    pe.wait_ge(yn_ready, i)
                    if live(n1):
                        pe.wait_ge(glo_ready2, 2 * n1 + 2)
                    elif live(i - 3):
                        pe.wait_ge(out_ready2, 2 * (i - 3) + 2)
                    transposes(yn[:, n1s, :], yT_mm2)
                if live(i):
                    outputs(i, m, 2)
                    scores(i, m, 3)
                if live(n1):
                    pe.wait_ge(klo_ready, n1 + 1)
                    if at(i, FIRST):
                        pe.wait_ge(wv_ready, 2)
                    if live(i - 1):
                        pe.wait_ge(yT_ready2, 2 * i)
                    else:
                        pe.wait_ge(glo_ready2, 2 * n1 + 2)
                    for k in range(2):
                        half = slice(k * BANK, (k + 1) * BANK)
                        nc.tensor.matmul(T[:, k, :], k_hi[:, n1s, :], wv_st[:, half], start=True, stop=False)
                        nc.tensor.matmul(T[:, k, :], k_lo[:, n1s, :], wv_st[:, half], start=False,
                                         stop=True).then_inc(v_mm2, 1)
                    maxima(n1, m + 1, 0)
                if live(i):
                    if live(n1):
                        pe.wait_ge(klo_ready, n1 + 1)
                    else:
                        pe.wait_ge(wlo_ready, i - 1)
                    outputs(i, m, 3)
                if live(n1):
                    maxima(n1, m + 1, 1)
                if live(i - 1):
                    if live(i):
                        pe.wait_ge(om_ready, i + 1)
                    else:
                        pe.wait_ge(wlo_ready, i - 1)
                    if at(i, 1):
                        pe.wait_ge(r_ready, 1)
                    experts(i - 1, 0)
                if live(n1):
                    maxima(n1, m + 1, 2)
                if live(i - 1):
                    experts(i - 1, 1)
                if live(n1):
                    maxima(n1, m + 1, 3)
                    pe.wait_ge(max_ready4, NG * n1 + NG)
                    if live(i - 1):
                        pe.wait_ge(h_ready, i)
                    elif live(i):
                        pe.wait_ge(om_ready, i + 1)
                    nc.tensor.transpose(M[0:H, 0:P], nmax[:], ident[:]).then_inc(nT_mm, 1)
                if live(i - 2):
                    pe.wait_ge(wlo_ready, i - 1)
                    if live(n1):
                        pe.wait_ge(v_ready2, 2 * n1 + 2)
                    elif live(i - 1):
                        pe.wait_ge(yT_ready2, 2 * i)
                    else:
                        pe.wait_ge(out_ready2, 2 * (i - 3) + 2)
                    for k in range(2):
                        half = slice(k * BANK, (k + 1) * BANK)
                        nc.tensor.matmul(T[:, k, :], w_hi[:], b_hi[:, half], start=True, stop=False)
                        nc.tensor.matmul(T[:, k, :], w_hi[:], b_lo[:, half], start=False, stop=False)
                        nc.tensor.matmul(T[:, k, :], w_lo[:], b_hi[:, half], start=False,
                                         stop=True).then_inc(f_mm2, 1)
                if at(i, FIRST):
                    pe.wait_ge(a_in, 32)
                    pe.wait_ge(v_ready2, 2)
                    transposes(a_f, a_tr)
                    pe.wait_ge(nT_ready, 1)
                    for c in range(C):
                        last = nc.tensor.transpose(M[:, c * NX:(c + 1) * NX], r_f[:, c * P:(c + 1) * P],
                                                   ident[0:NX, 0:NX])
                    last.then_inc(r_tr, 1)
                    pe.wait_ge(b_in, 16 * C)
                    pe.wait_ge(a_ready, 2)
                    transposes(b_f[:].rearrange("p c e r -> p (c e r)"), b_tr)
                    pe.wait_ge(r_ready, 1)
                    pe.wait_ge(b_ready, 2)
                if live(n1):
                    scores(n1, m + 1, 0)

            pe.wait_ge(consts, 1 + 1 + NX + 1)
            pe.wait_ge(wq_in, 16)
            pe.wait_ge(wkv_in, 32)
            pe.wait_ge(wqk_ready, 2)
            pipeline(pe, iteration)


_INS = ['x', 'ctx_4096', 'L0_xattn_Wq_d', 'L0_xattn_W_qk', 'L0_xattn_Wkv_d', 'L0_xattn_Wv_u',
        'L0_ffn_route_w', 'L0_ffn_A', 'L0_ffn_Bw']
_OUTS = [((16, 128, 1024), 'float32')]


def kernel(**inputs):
    import numpy as _np
    import concourse.bacc as _bacc
    from concourse import mybir as _mybir
    from concourse.bass_utils import run_bass_kernel_spmd as _run

    nc = _bacc.Bacc("TRN2", target_bir_lowering=False, num_devices=1)
    arrays, args = {}, []
    for name in _INS:
        a = _np.ascontiguousarray(inputs[name])
        arrays[f"in_{name}_dram"] = a
        args.append(nc.dram_tensor(f"in_{name}_dram", a.shape, _mybir.dt.from_np(a.dtype), kind="ExternalInput").ap())
    for i, (shape, dtype) in enumerate(_OUTS):
        dt = _mybir.dt.from_np(_np.dtype(dtype))
        args.append(nc.dram_tensor(f"out_{i}_dram", shape, dt, kind="ExternalOutput").ap())
    xattn_ffn_kernel(nc, *args)
    r = _run(nc, [arrays], core_ids=[0])
    return r.results[0]["out_0_dram"]
```

```python
import concourse.bass as bass
from concourse import mybir
from contextlib import ExitStack



def xattn_ffn_kernel(nc, x, ctx_in, w_q, w_qk, w_kv, w_v, route_w, a_w, b_w, out):
    f32, f16 = mybir.dt.float32, mybir.dt.float16
    ALU, ACT, AX = mybir.AluOpType, mybir.ActivationFunctionType, mybir.AxisListType

    NB, P, E = x.shape
    LQ = w_q.shape[1]
    L = w_kv.shape[1]
    H = w_qk.shape[1] // L
    HD = w_v.shape[1] // H
    NX, R, _ = a_w.shape
    ER = NX * R
    HR = ER + NX
    C = E // P
    HC = C // 2
    BANK = 512
    G4 = 4
    NG = H // G4
    OB = BANK // (HD + 1)
    OM = H - 2 * OB
    EPS = 1e-5
    WS = 16.0
    KS = 32.0
    BS = 64.0
    MS = 64.0
    SOFT = 1.0 / (WS * L ** 0.5)
    FS = 1.0 / (WS * BS)
    RING = 4
    FIRST, LAST, LOOP = -1, NB + 1, (4, NB - 4)

    with ExitStack() as stack:
        def sb(name, shape, dt):
            return stack.enter_context(nc.sbuf_tensor(name, shape, dt))

        def pb(name, shape):
            return stack.enter_context(nc.psum_tensor(name, shape, f32))

        def sem(name):
            return stack.enter_context(nc.semaphore(name))

        wq = sb("wq", [P, C, LQ], f32)
        wkv_f = sb("wkv_f", [P, C, L], f32)
        wkv_hi = sb("wkv_hi", [P, C, L], f16)
        wkv_lo = sb("wkv_lo", [P, C, L], f16)
        wqk_f = sb("wqk_f", [P, C, 2, L], f32)
        wqk_hi = sb("wqk_hi", [P, C, 2 * L], f16)
        wqk_lo = sb("wqk_lo", [P, C, 2 * L], f16)
        wv_f = sb("wv_f", [P, E], f32)
        wv_hi = sb("wv_hi", [P, E], f16)
        wv_st = sb("wv_st", [P, E], f16)
        a_f = sb("a_f", [P, E], f32)
        r_f = sb("r_f", [NX, E], f32)
        ar = sb("ar", [P, C, HR], f32)
        b_f = sb("b_f", [P, C, NX, R], f32)
        b_hi = sb("b_hi", [P, E], f16)
        b_lo = sb("b_lo", [P, E], f16)
        ident = sb("ident", [P, P], f32)
        pick = sb("pick", [H, H, P], f16)
        prefer = sb("prefer", [P, NX], f32)
        mhalf = sb("mhalf", [P, 1], f32)
        x_sb = sb("x_sb", [P, RING, E], f32)
        c_sb = sb("c_sb", [P, RING, E], f32)
        xn = sb("xn", [P, 2, E], f32)
        xT = sb("xT", [P, C, P], f32)
        c_hi = sb("c_hi", [P, C, P], f16)
        c_lo = sb("c_lo", [P, C, P], f16)
        k_f = sb("k_f", [P, 2, L], f32)
        q_hi = sb("q_hi", [P, P], f16)
        q_lo = sb("q_lo", [P, P], f16)
        k_hi = sb("k_hi", [P, 2, P], f16)
        k_lo = sb("k_lo", [P, 2, P], f16)
        g_hi = sb("g_hi", [P, 2, C, P], f16)
        g_lo = sb("g_lo", [P, 2, C, P], f16)
        v_hi = sb("v_hi", [P, 2, H, HD + 1], f16)
        v_lo = sb("v_lo", [P, 2, H, HD + 1], f16)
        nmax = sb("nmax", [P, H], f32)
        nmaxT = sb("nmaxT", [H, P], f16)
        prob = sb("prob", [P, NG, BANK], f32)
        p_hi = sb("p_hi", [P, NG, BANK], f16)
        p_lo = sb("p_lo", [P, NG, BANK], f16)
        rsum = sb("rsum", [P, H], f32)
        o_sb = sb("o_sb", [P, 2, E], f32)
        y_sb = sb("y_sb", [P, RING, E], f32)
        yn = sb("yn", [P, 2, E], f32)
        yT = sb("yT", [P, C, P], f32)
        h_sb = sb("h_sb", [P, HR], f32)
        top = sb("top", [P, 4], f32)
        tie = sb("tie", [P, NX], f32)
        rw = sb("rw", [P, NX], f32)
        wh = sb("wh", [P, NX, R], f32)
        w_hi = sb("w_hi", [P, P], f16)
        w_lo = sb("w_lo", [P, P], f16)
        o_out = sb("o_out", [P, 2, E], f32)
        bn = sb("bn", [P, 2, 2, 6], f32)
        mv = sb("mv", [P, 2, 2, 2], f32)
        ln = sb("ln", [P, 2, 3], f32)

        T = pb("T", [P, 2, BANK])
        S = pb("S", [P, BANK])
        D = pb("D", [P, 2, BANK])
        O = pb("O", [P, 2, BANK])
        M = pb("M", [P, BANK])

        x_in = [sem(f"x_in{n}") for n in range(RING)]
        c_in = [sem(f"c_in{n}") for n in range(RING)]
        wq_in, wkv_in, wqk_in, wv_in, a_in, b_in = (sem(n) for n in (
            "wq_in", "wkv_in", "wqk_in", "wv_in", "a_in", "b_in"))
        consts, apart = sem("consts"), sem("apart")
        wqk_ready, wvh_ready, wv_ready = sem("wqk_ready"), sem("wvh_ready"), sem("wv_ready")
        a_tr, a_ready, r_tr, r_ready = sem("a_tr"), sem("a_ready"), sem("r_tr"), sem("r_ready")
        b_tr, bhi_ready, b_ready = sem("b_tr"), sem("bhi_ready"), sem("b_ready")
        x_bn2, y_bn2, x_stat, y_stat = sem("x_bn2"), sem("y_bn2"), sem("x_stat"), sem("y_stat")
        x_ln, y_ln = sem("x_ln"), sem("y_ln")
        xn_ready, yn_ready, y_ready2 = sem("xn_ready"), sem("yn_ready"), sem("y_ready2")
        xT_mm2, xT_ready2 = sem("xT_mm2"), sem("xT_ready2")
        cT_mm2, chi_ready2, clo_ready2 = sem("cT_mm2"), sem("chi_ready2"), sem("clo_ready2")
        wkv_ready, k_mm, k_ready = sem("wkv_ready"), sem("k_mm"), sem("k_ready")
        yT_mm2, yT0_ready, yT1_ready = sem("yT_mm2"), sem("yT0_ready"), sem("yT1_ready")
        q_mm, qhi_ready, qlo_ready = sem("q_mm"), sem("qhi_ready"), sem("qlo_ready")
        kT_mm, khi_ready, klo_ready = sem("kT_mm"), sem("khi_ready"), sem("klo_ready")
        g_mm2, ghi_ready2, glo_ready2 = sem("g_mm2"), sem("ghi_ready2"), sem("glo_ready2")
        v_mm2, vhi_ready2, vlo_ready2 = sem("v_mm2"), sem("vhi_ready2"), sem("vlo_ready2")
        s_mm4, max_ready4 = sem("s_mm4"), sem("max_ready4")
        nT_mm, nT_ready = sem("nT_mm"), sem("nT_ready")
        d_mm4, phi_ready4, exp_ready4, plo_ready4 = sem("d_mm4"), sem("phi_ready4"), sem("exp_ready4"), sem("plo_ready4")
        pv_mm4, om_ready, o_ready = sem("pv_mm4"), sem("om_ready"), sem("o_ready")
        h_mm, h_ready, wh_ready = sem("h_mm"), sem("h_ready"), sem("wh_ready")
        wT_mm, whi_ready, wlo_ready = sem("wT_mm"), sem("whi_ready"), sem("wlo_ready")
        f_mm2, out_ready2 = sem("f_mm2"), sem("out_ready2")
        stored = [sem(f"stored{n}") for n in range(2)]
        o_step2, route4, pool_chain = sem("o_step2"), sem("route4"), sem("pool_chain")

        def live(b):
            return not isinstance(b, int) or 0 <= b < NB

        def at(i, n):
            return isinstance(i, int) and i == n

        def wait(eng, s, n):
            if not isinstance(n, int) or n > 0:
                eng.wait_ge(s, n)

        def wait_apart(eng, s, n):
            wait(eng, s, n)
            eng.sem_inc(apart, 1)

        def arrived(eng, s, b, m, ring):
            eng.wait_ge(s[m], (16 // ring) * (b - m) + 16)

        def pipeline(eng, iteration, first=FIRST, loop=LOOP, last=LAST):
            for i in range(first, loop[0]):
                iteration(i, i % RING)
            with eng.Fori(loop[0], loop[1] - RING + 1, RING) as i0:
                for n in range(RING):
                    iteration(i0 + n, (loop[0] + n) % RING)
            for i in range(loop[1], last + 1):
                iteration(i, i % RING)

        block = stack.enter_context(nc.Block())

        @block.sync
        def _(sp):
            def load(b, m):
                sp.dma_start(x_sb[:, m, :], x[b, :, :]).then_inc(x_in[m], 16)
                sp.dma_start(c_sb[:, m, :], ctx_in[b, :, :]).then_inc(c_in[m], 16)

            load(0, 0)
            sp.dma_start(wq[:], w_q.rearrange("(c p) n -> p c n", p=P)).then_inc(wq_in, 16)
            sp.dma_start(wkv_f[:], w_kv.rearrange("(c p) n -> p c n", p=P)).then_inc(wkv_in, 16)
            qk = w_qk.rearrange("p (t c l) -> p t c l", t=2, l=L)
            for t in range(2):
                sp.dma_start(wqk_f[:, :, t, :], qk[:, t, :, :]).then_inc(wqk_in, 16)
            for t in range(2):
                sp.dma_start(wv_f[t * L:(t + 1) * L, :], w_v).then_inc(wv_in, 16)
            load(1, 1)
            sp.dma_start(a_f[:], a_w.rearrange("e r d -> (e r) d")).then_inc(a_in, 16)
            sp.dma_start(r_f[:], route_w).then_inc(a_in, 16)
            load(2, 2)
            bw = b_w.rearrange("e (c p) r -> p c e r", p=P)
            for c in range(C):
                sp.dma_start(b_f[:, c, :, :], bw[:, c, :, :]).then_inc(b_in, 16)

            def iteration(i, m):
                b = i + 3
                if live(b):
                    wait(sp, y_stat, i)
                    load(b, (m + 3) % RING)
                b = i - 2
                if live(b):
                    sp.wait_ge(out_ready2, 2 * b + 2)
                    sp.dma_start(out[b, :, :], o_out[:, m % 2, :]).then_inc(stored[m % 2], 16)

            pipeline(sp, iteration, first=0, loop=(2, 10))
            for n in range(2):
                sp.wait_ge(stored[n], 16 * (NB // 2))

        @block.gpsimd
        def _(pool):
            chain = [0]

            def link(ins):
                chain[0] += 1
                ins.then_inc(pool_chain, 1)
                pool.wait_ge(pool_chain, chain[0])

            link(nc.gpsimd.memset(ident[:], 0.0))
            nc.gpsimd.affine_select(out=ident[:], in_=ident[:], compare_op=ALU.not_equal, fill=1.0, base=0,
                                    pattern=[[-1, P]], channel_multiplier=1).then_inc(consts, 1)
            link(nc.gpsimd.memset(mhalf[:], -0.5))
            link(nc.gpsimd.memset(pick[:], 0.0))
            nc.gpsimd.affine_select(out=pick[:], in_=pick[:], compare_op=ALU.not_equal, fill=MS, base=0,
                                    pattern=[[-1, H], [0, P]], channel_multiplier=1).then_inc(consts, 1)
            for e in range(NX):
                nc.gpsimd.memset(prefer[:, e:e + 1], float(NX - e)).then_inc(consts, 1)
            nc.gpsimd.memset(v_hi[:, :, :, HD:HD + 1], WS).then_inc(consts, 1)
            nc.gpsimd.memset(v_lo[:, :, :, HD:HD + 1], 0.0).then_inc(consts, 1)

            def normalise(dst, src, stat, which, b, ln_step, done):
                wait_apart(pool, done, b)
                part = ln[:, which, :]
                nc.gpsimd.tensor_scalar(part[:, 1:2], stat[:, 1:2], 1.0, EPS, ALU.mult, ALU.add).then_inc(ln_step, 1)
                nc.gpsimd.tensor_scalar(part[:, 0:1], stat[:, 0:1], -1.0, 0.0, ALU.mult, ALU.add).then_inc(ln_step, 1)
                wait_apart(pool, ln_step, 3 * b + 1)
                nc.gpsimd.tensor_tensor(part[:, 2:3], part[:, 1:2], mhalf[:], ALU.pow).then_inc(ln_step, 1)
                wait_apart(pool, ln_step, 3 * b + 3)
                nc.gpsimd.tensor_scalar(dst, src, part[:, 0:1], part[:, 2:3], ALU.add, ALU.mult).then_inc(done, 1)

            def iteration(i, m):
                def low(g):
                    pool.wait_ge(exp_ready4, NG * i + g + 1)
                    wait(pool, pv_mm4, NG * (i - 1) + g + 1)
                    nc.gpsimd.tensor_tensor(p_lo[:, g, :], prob[:, g, :], p_hi[:, g, :],
                                            ALU.subtract).then_inc(plo_ready4, 1)

                if live(i):
                    low(0)
                b = i - 1
                if live(b):
                    pool.wait_ge(o_ready, b + 1)
                    wait(pool, out_ready2, 2 * (b - 1))
                    for k in range(2):
                        half = slice(k * BANK, (k + 1) * BANK)
                        nc.gpsimd.tensor_tensor(y_sb[:, (m - 1) % RING, half], x_sb[:, (m - 1) % RING, half],
                                                o_sb[:, (m - 1) % 2, half], ALU.add).then_inc(y_ready2, 1)
                if live(i):
                    low(1)
                if live(b):
                    pool.wait_ge(y_stat, b + 1)
                    wait(pool, yT_mm2, 2 * (b - 1))
                    normalise(yn[:, (m - 1) % 2, :], y_sb[:, (m - 1) % RING, :], mv[:, 1, (m - 1) % 2, :],
                              1, b, y_ln, yn_ready)
                if live(i):
                    low(2)
                b = i + 2
                if live(b):
                    pool.wait_ge(x_stat, b + 1)
                    wait(pool, xT_mm2, 2 * (b - 1))
                    normalise(xn[:, m % 2, :], x_sb[:, (m + 2) % RING, :], mv[:, 0, m % 2, :],
                              0, b, x_ln, xn_ready)
                if live(i):
                    low(3)

            pipeline(pool, iteration, first=FIRST - 1)

        @block.vector
        def _(dve):
            dve.wait_ge(wkv_in, 16)
            dve.wait_ge(wkv_ready, 1)
            nc.vector.scalar_tensor_tensor(wkv_lo[:], wkv_f[:], KS, wkv_hi[:],
                                           ALU.mult, ALU.subtract).then_inc(wkv_ready, 1)
            dve.wait_ge(wqk_in, 32)
            dve.wait_ge(wqk_ready, 1)
            nc.vector.scalar_tensor_tensor(wqk_lo[:], wqk_f[:].rearrange("p c t l -> p c (t l)"), WS, wqk_hi[:],
                                           ALU.mult, ALU.subtract).then_inc(wqk_ready, 1)
            dve.wait_ge(wv_in, 32)
            dve.wait_ge(wvh_ready, 1)
            nc.vector.scalar_tensor_tensor(wv_st[L:P, :], wv_f[L:P, :], WS, wv_hi[L:P, :],
                                           ALU.mult, ALU.subtract).then_inc(wv_ready, 1)

            def half_statistics(src, which, b, k, step, done):
                if k == 0:
                    wait(dve, done, b)
                nc.vector.bn_stats(bn[:, which, k, :], src[:, k * BANK:(k + 1) * BANK]).then_inc(step, 1)

            def statistics(which, b, slot, step, done):
                wait_apart(dve, step, 2 * b + 2)
                nc.vector.bn_aggr(mv[:, which, slot, :], bn[:, which, :, :]).then_inc(done, 1)

            def iteration(i, m):
                def maximum(g):
                    dve.wait_ge(s_mm4, NG * (i + 1) + g + 1)
                    h0 = C * (g % 2) + G4 * (g // 2)
                    nc.vector.tensor_reduce(nmax[:, h0:h0 + G4], S[:].rearrange("p (h t) -> p h t", t=P),
                                            AX.X, ALU.max, negate=True).then_inc(max_ready4, 1)

                b = i - 1
                if live(b):
                    dve.wait_ge(pv_mm4, NG * b + NG)
                    wait(dve, y_ready2, 2 * (b - 1))
                    om = S[:, 0:OM * (HD + 1)].rearrange("p (h d) -> p h d", h=OM)
                    oe = O[:, :, 0:OB * (HD + 1)].rearrange("p k (h d) -> p k h d", h=OB)
                    slot = o_sb[:, (m - 1) % 2, :]
                    nc.vector.reciprocal(rsum[:, 2 * OB:H], om[:, :, HD]).then_inc(o_step2, 1)
                    re = rsum[:, 0:2 * OB].rearrange("p (k h) -> p k h", k=2)
                    nc.vector.reciprocal(re, oe[:, :, :, HD]).then_inc(o_step2, 1)
                    dve.wait_ge(o_step2, 2 * b + 2)
                    nc.vector.tensor_tensor(
                        slot[:, 2 * OB * HD:E].rearrange("p (h d) -> p h d", h=OM), om[:, :, 0:HD],
                        rsum[:, 2 * OB:H].unsqueeze(2).broadcast_to([P, OM, HD]), ALU.mult).then_inc(om_ready, 1)
                    nc.vector.tensor_tensor(
                        slot[:, 0:2 * OB * HD].rearrange("p (k h d) -> p k h d", k=2, h=OB), oe[:, :, :, 0:HD],
                        re.unsqueeze(3).broadcast_to([P, 2, OB, HD]), ALU.mult).then_inc(o_ready, 1)
                b = i - 2
                if live(b):
                    dve.wait_ge(whi_ready, b + 1)
                    wait(dve, f_mm2, 2 * b)
                    nc.vector.scalar_tensor_tensor(w_lo[:], M[:, 0:P], WS, w_hi[:], ALU.mult,
                                                   ALU.subtract).then_inc(wlo_ready, 1)
                b = i + 2
                if live(b):
                    arrived(dve, x_in, b, (m + 2) % RING, RING)
                    wait(dve, xn_ready, b - 1)
                    for k in range(2):
                        half_statistics(x_sb[:, (m + 2) % RING, :], 0, b, k, x_bn2, x_stat)
                    statistics(0, b, m % 2, x_bn2, x_stat)
                b = i - 1
                if live(b):
                    dve.wait_ge(y_ready2, 2 * b + 1)
                    half_statistics(y_sb[:, (m - 1) % RING, :], 1, b, 0, y_bn2, y_stat)
                b, s = i + 1, (m + 1) % 2
                if live(b):
                    wait(dve, k_mm, b)
                    for k in range(2):
                        dve.wait_ge(chi_ready2, 2 * b + k + 1)
                        nc.vector.tensor_tensor(c_lo[:, k * HC:(k + 1) * HC, :], T[:, k, :].rearrange(
                            "p (j t) -> p j t", t=P), c_hi[:, k * HC:(k + 1) * HC, :],
                            ALU.subtract).then_inc(clo_ready2, 1)
                    dve.wait_ge(qhi_ready, b + 1)
                    wait(dve, g_mm2, 2 * b)
                    nc.vector.tensor_tensor(q_lo[:], M[:, 0:P], q_hi[:], ALU.subtract).then_inc(qlo_ready, 1)
                b = i - 1
                if live(b):
                    dve.wait_ge(y_ready2, 2 * b + 2)
                    half_statistics(y_sb[:, (m - 1) % RING, :], 1, b, 1, y_bn2, y_stat)
                    wait(dve, yn_ready, b - 1)
                    statistics(1, b, (m - 1) % 2, y_bn2, y_stat)
                b = i + 1
                if live(b):
                    wait(dve, d_mm4, NG * (b - 1))
                    for k in range(2):
                        dve.wait_ge(ghi_ready2, 2 * b + k + 1)
                        nc.vector.tensor_tensor(g_lo[:, s, k * HC:(k + 1) * HC, :], T[:, k, :].rearrange(
                            "p (j t) -> p j t", t=P), g_hi[:, s, k * HC:(k + 1) * HC, :],
                            ALU.subtract).then_inc(glo_ready2, 1)
                    dve.wait_ge(khi_ready, b + 1)
                    nc.vector.tensor_tensor(k_lo[:, s, :], M[:, 0:P], k_hi[:, s, :],
                                            ALU.subtract).then_inc(klo_ready, 1)
                if live(i + 1):
                    wait(dve, nT_mm, i + 1)
                    maximum(0)
                b = i - 1
                if live(b):
                    dve.wait_ge(yT_mm2, 2 * b + 2)
                    wait(dve, h_mm, b)
                    nc.vector.tensor_copy(yT[:, HC:C, :], T[:, 1, :].rearrange(
                        "p (j t) -> p j t", t=P)).then_inc(yT1_ready, 1)
                b = i + 1
                if live(b):
                    maximum(1)
                    maximum(2)
                    wait(dve, pv_mm4, NG * (b - 1))
                    for k in range(2):
                        dve.wait_ge(vhi_ready2, 2 * b + k + 1)
                        hs = slice(k * (H // 2), (k + 1) * (H // 2))
                        nc.vector.tensor_tensor(v_lo[:, s, hs, 0:HD], T[:, k, :].rearrange(
                            "p (h d) -> p h d", d=HD), v_hi[:, s, hs, 0:HD], ALU.subtract).then_inc(vlo_ready2, 1)
                    maximum(3)
                b = i - 1
                if live(b):
                    dve.wait_ge(h_ready, b + 1)
                    wait(dve, wT_mm, b)
                    logits = h_sb[:, ER:HR]
                    nc.vector.tensor_reduce(top[:, 0:1], logits, AX.X, ALU.max).then_inc(route4, 1)
                    dve.wait_ge(route4, 4 * b + 1)
                    nc.vector.scalar_tensor_tensor(tie[:], logits, top[:, 0:1], prefer[:], ALU.is_equal,
                                                   ALU.mult).then_inc(route4, 1)
                    dve.wait_ge(route4, 4 * b + 2)
                    nc.vector.tensor_reduce(top[:, 1:2], tie[:], AX.X, ALU.max).then_inc(route4, 1)
                    dve.wait_ge(route4, 4 * b + 3)
                    nc.vector.tensor_scalar(rw[:], tie[:], top[:, 1:2], top[:, 0:1], ALU.is_equal,
                                            ALU.mult).then_inc(route4, 1)
                    dve.wait_ge(route4, 4 * b + 4)
                    nc.vector.tensor_tensor(wh[:], h_sb[:, 0:ER].rearrange("p (e r) -> p e r", e=NX),
                                            rw[:].unsqueeze(2).broadcast_to([P, NX, R]),
                                            ALU.mult).then_inc(wh_ready, 1)
                b = i - 2
                if live(b):
                    wait(dve, stored[m % 2], 8 * (b - m % 2))
                    for k in range(2):
                        dve.wait_ge(f_mm2, 2 * b + k + 1)
                        half = slice(k * BANK, (k + 1) * BANK)
                        nc.vector.scalar_tensor_tensor(o_out[:, m % 2, half], T[:, k, :], FS,
                                                       y_sb[:, (m - 2) % RING, half], ALU.mult,
                                                       ALU.add).then_inc(out_ready2, 1)
                if at(i, FIRST):
                    for k in range(2):
                        dve.wait_ge(bhi_ready, k + 1)
                        half = slice(k * BANK, (k + 1) * BANK)
                        nc.vector.scalar_tensor_tensor(b_lo[:, half], T[:, k, :], BS, b_hi[:, half], ALU.mult,
                                                       ALU.subtract).then_inc(b_ready, 1)

            dve.wait_ge(consts, 1 + 1 + NX + 2)
            pipeline(dve, iteration, first=FIRST - 1)

        @block.scalar
        def _(act):
            act.wait_ge(wkv_in, 16)
            nc.scalar.activation(wkv_hi[:], wkv_f[:], ACT.Copy, scale=KS).then_inc(wkv_ready, 1)
            act.wait_ge(wqk_in, 32)
            nc.scalar.activation(wqk_hi[:], wqk_f[:].rearrange("p c t l -> p c (t l)"), ACT.Copy,
                                 scale=WS).then_inc(wqk_ready, 1)
            act.wait_ge(wv_in, 32)
            nc.scalar.activation(wv_hi[L:P, :], wv_f[L:P, :], ACT.Copy, scale=WS).then_inc(wvh_ready, 1)
            nc.scalar.activation(wv_st[0:L, :], wv_f[0:L, :], ACT.Copy, scale=WS).then_inc(wv_ready, 1)

            def copy_out(dst, mm, free, free_n, done, b):
                wait(act, free, free_n)
                for k in range(2):
                    act.wait_ge(mm, 2 * b + k + 1)
                    nc.scalar.activation(dst[:, k * HC:(k + 1) * HC, :], T[:, k, :].rearrange(
                        "p (j t) -> p j t", t=P), ACT.Copy).then_inc(done, 1)

            def exps(b, g, between=None):
                act.wait_ge(d_mm4, NG * b + g + 1)
                wait(act, pv_mm4, NG * (b - 1) + g + 1)
                nc.scalar.activation(p_hi[:, g, :], D[:, g % 2, :], ACT.Exp, scale=SOFT).then_inc(phi_ready4, 1)
                if between:
                    between()
                nc.scalar.activation(prob[:, g, :], D[:, g % 2, :], ACT.Exp, scale=SOFT).then_inc(exp_ready4, 1)

            def iteration(i, m):
                s = (m + 1) % 2
                b = i - 2
                if live(b):
                    act.wait_ge(wT_mm, b + 1)
                    wait(act, f_mm2, 2 * b)
                    nc.scalar.activation(w_hi[:], M[:, 0:P], ACT.Copy, scale=WS).then_inc(whi_ready, 1)
                if live(i + 1):
                    copy_out(xT, xT_mm2, q_mm, i + 1, xT_ready2, i + 1)
                if live(i):
                    exps(i, 1)
                b = i + 1
                if live(b):
                    copy_out(c_hi, cT_mm2, k_mm, b, chi_ready2, b)
                    act.wait_ge(q_mm, b + 1)
                    wait(act, g_mm2, 2 * b)
                    nc.scalar.activation(q_hi[:], M[:, 0:P], ACT.Copy).then_inc(qhi_ready, 1)
                if live(i):
                    exps(i, 2)
                if live(b):
                    act.wait_ge(k_mm, b + 1)
                    wait(act, kT_mm, b)
                    nc.scalar.activation(k_f[:], M[:, 0:L].unsqueeze(1).broadcast_to([P, 2, L]), ACT.Copy,
                                         scale=1.0 / KS).then_inc(k_ready, 1)
                    wait(act, d_mm4, NG * (b - 1))
                    wait(act, v_mm2, 2 * (b - 1))
                    for k in range(2):
                        act.wait_ge(g_mm2, 2 * b + k + 1)
                        nc.scalar.activation(g_hi[:, s, k * HC:(k + 1) * HC, :], T[:, k, :].rearrange(
                            "p (j t) -> p j t", t=P), ACT.Copy).then_inc(ghi_ready2, 1)
                    act.wait_ge(kT_mm, b + 1)
                    nc.scalar.activation(k_hi[:, s, :], M[:, 0:P], ACT.Copy).then_inc(khi_ready, 1)

                def copy_yT0():
                    act.wait_ge(yT_mm2, 2 * i - 1)
                    wait(act, h_mm, i - 1)
                    nc.scalar.activation(yT[:, 0:HC, :], T[:, 0, :].rearrange(
                        "p (j t) -> p j t", t=P), ACT.Copy).then_inc(yT0_ready, 1)

                if live(i):
                    exps(i, 3, copy_yT0 if live(i - 1) else None)
                elif live(i - 1):
                    copy_yT0()
                if live(b):
                    wait(act, pv_mm4, NG * (b - 1))
                    for k in range(2):
                        act.wait_ge(v_mm2, 2 * b + k + 1)
                        nc.scalar.activation(v_hi[:, s, k * (H // 2):(k + 1) * (H // 2), 0:HD], T[:, k, :].rearrange(
                            "p (h d) -> p h d", d=HD), ACT.Copy).then_inc(vhi_ready2, 1)
                if live(i - 1):
                    act.wait_ge(h_mm, i)
                    wait(act, wh_ready, i - 1)
                    nc.scalar.activation(h_sb[:], M[:, 0:HR], ACT.Copy).then_inc(h_ready, 1)
                if live(b):
                    act.wait_ge(nT_mm, b + 1)
                    wait(act, d_mm4, NG * b)
                    nc.scalar.activation(nmaxT[:], M[0:H, 0:P], ACT.Copy, scale=1.0 / MS).then_inc(nT_ready, 1)
                if at(i, FIRST):
                    for k in range(2):
                        act.wait_ge(a_tr, k + 1)
                        nc.scalar.activation(ar[:, k * HC:(k + 1) * HC, 0:ER], T[:, k, :].rearrange(
                            "p (j t) -> p j t", t=P), ACT.Copy).then_inc(a_ready, 1)
                    act.wait_ge(r_tr, 1)
                    nc.scalar.activation(ar[:, :, ER:HR], M[:, 0:C * NX].rearrange("p (c e) -> p c e", e=NX),
                                         ACT.Copy).then_inc(r_ready, 1)
                    for k in range(2):
                        act.wait_ge(b_tr, k + 1)
                        nc.scalar.activation(b_hi[:, k * BANK:(k + 1) * BANK], T[:, k, :], ACT.Copy,
                                             scale=BS).then_inc(bhi_ready, 1)
                if live(b):
                    exps(b, 0)

            pipeline(act, iteration)

        @block.tensor
        def _(pe):
            def transposes(src, mm, free=None):
                for c in range(C):
                    if c % HC == 0 and free:
                        free(c // HC)
                    last = nc.tensor.transpose(T[:, c // HC, (c % HC) * P:(c % HC + 1) * P],
                                               src[:, c * P:(c + 1) * P], ident[:])
                    if c % HC == HC - 1:
                        last.then_inc(mm, 1)

            def scores(b, m, g):
                if g == 0:
                    pe.wait_ge(klo_ready, b + 1)
                    pe.wait_ge(glo_ready2, 2 * b + 2)
                wait(pe, exp_ready4, NG * b + g - 1)
                s, j0 = m % 2, G4 * (g // 2)
                rows = slice(L * (g % 2), L * (g % 2 + 1))
                d = D[:, g % 2, :]
                hi = g_hi[rows, s, j0:j0 + G4, :].rearrange("p j t -> p (j t)")
                lo = g_lo[rows, s, j0:j0 + G4, :].rearrange("p j t -> p (j t)")
                nc.tensor.matmul(d, k_hi[rows, s, :], hi, start=True, stop=False)
                nc.tensor.matmul(d, k_hi[rows, s, :], lo, start=False, stop=False)
                nc.tensor.matmul(d, k_lo[rows, s, :], hi, start=False, stop=False)
                if g == 0:
                    pe.wait_ge(nT_ready, b + 1)
                for n in range(G4):
                    last = nc.tensor.matmul(d[:, n * P:(n + 1) * P], pick[:, C * (g % 2) + j0 + n, :], nmaxT[:],
                                            start=False, stop=(n == G4 - 1))
                last.then_inc(d_mm4, 1)

            def outputs(b, m, g):
                if g == 0:
                    pe.wait_ge(vlo_ready2, 2 * b + 2)
                    wait(pe, o_ready, b)
                if g == NG - 1 and live(b + 1):
                    pe.wait_ge(max_ready4, NG * (b + 1) + NG)
                pe.wait_ge(plo_ready4, NG * b + g + 1)
                for n in range(G4):
                    h = C * (g % 2) + G4 * (g // 2) + n
                    bank = S if h >= 2 * OB else O[:, h // OB, :]
                    col = (h % OB) * (HD + 1)
                    o = bank[:, col:col + HD + 1]
                    hi, lo = p_hi[:, g, n * P:(n + 1) * P], p_lo[:, g, n * P:(n + 1) * P]
                    nc.tensor.matmul(o, hi, v_hi[:, m % 2, h, :], start=True, stop=False)
                    nc.tensor.matmul(o, hi, v_lo[:, m % 2, h, :], start=False, stop=False)
                    last = nc.tensor.matmul(o, lo, v_hi[:, m % 2, h, :], start=False, stop=True)
                last.then_inc(pv_mm4, 1)

            def maxima(b, m, g):
                if g == 0:
                    pe.wait_ge(khi_ready, b + 1)
                    pe.wait_ge(ghi_ready2, 2 * b + 2)
                wait(pe, max_ready4, NG * b + g)
                if g == 0:
                    wait(pe, om_ready, b - 1)
                rows = slice(L * (g % 2), L * (g % 2 + 1))
                for n in range(G4):
                    last = nc.tensor.matmul(S[:, n * P:(n + 1) * P], g_hi[rows, m % 2, G4 * (g // 2) + n, :],
                                            k_hi[rows, m % 2, :], start=True, stop=True)
                last.then_inc(s_mm4, 1)

            def experts(b, k):
                pe.wait_ge(yT1_ready if k else yT0_ready, b + 1)
                for c in range(k * HC, (k + 1) * HC):
                    last = nc.tensor.matmul(M[:, 0:HR], yT[:, c, :], ar[:, c, :], start=(c == 0), stop=(c == C - 1))
                if k == 1:
                    last.then_inc(h_mm, 1)

            def iteration(i, m):
                n1, n1s = i + 1, (m + 1) % 2
                b = i - 2
                if live(b):
                    pe.wait_ge(wh_ready, b + 1)
                    if live(i):
                        pe.wait_ge(nT_ready, i + 1)
                    else:
                        wait(pe, h_ready, min(i - 1, NB))
                    nc.tensor.transpose(M[:, 0:P], wh[:].rearrange("p e r -> p (e r)"), ident[:]).then_inc(wT_mm, 1)
                if live(n1):
                    pe.wait_ge(xn_ready, n1 + 1)

                    def free(k):
                        wait(pe, vlo_ready2, 2 * i + k + 1)
                        if not isinstance(i, int) or i >= 3:
                            pe.wait_ge(out_ready2, 2 * (i - 3) + k + 1)

                    transposes(xn[:, n1s, :], xT_mm2, None if at(i, FIRST) else free)
                if live(i):
                    scores(i, m, 1)
                if live(n1):
                    arrived(pe, c_in, n1, (m + 1) % RING, RING)
                    transposes(c_sb[:, (m + 1) % RING, :], cT_mm2,
                               lambda k: pe.wait_ge(xT_ready2, 2 * n1 + k + 1))
                    if live(i - 2):
                        pe.wait_ge(wlo_ready, i - 1)
                    else:
                        wait(pe, nT_ready, n1)
                    for c in range(C):
                        last = nc.tensor.matmul(M[:, 0:P], wq[:, c, :], xT[:, c, :], start=(c == 0), stop=(c == C - 1))
                    last.then_inc(q_mm, 1)
                if live(i):
                    outputs(i, m, 0)
                    scores(i, m, 2)
                if live(n1):
                    pe.wait_ge(clo_ready2, 2 * n1 + 2)
                    pe.wait_ge(qlo_ready, n1 + 1)
                    for c in range(C):
                        k = M[:, 0:L]
                        nc.tensor.matmul(k, c_hi[:, c, :], wkv_hi[:, c, :], start=(c == 0), stop=False)
                        nc.tensor.matmul(k, c_hi[:, c, :], wkv_lo[:, c, :], start=False, stop=False)
                        last = nc.tensor.matmul(k, c_lo[:, c, :], wkv_hi[:, c, :], start=False, stop=(c == C - 1))
                    last.then_inc(k_mm, 1)
                    for j in range(C):
                        g = T[:, j // HC, (j % HC) * P:(j % HC + 1) * P]
                        nc.tensor.matmul(g, wqk_hi[:, j, :], q_hi[:], start=True, stop=False)
                        nc.tensor.matmul(g, wqk_hi[:, j, :], q_lo[:], start=False, stop=False)
                        last = nc.tensor.matmul(g, wqk_lo[:, j, :], q_hi[:], start=False, stop=True)
                        if j % HC == HC - 1:
                            last.then_inc(g_mm2, 1)
                    pe.wait_ge(k_ready, n1 + 1)
                    nc.tensor.transpose(M[:, 0:P], k_f[:].rearrange("p t l -> p (t l)"), ident[:]).then_inc(kT_mm, 1)
                if live(i):
                    outputs(i, m, 1)
                    scores(i, m, 3)
                if live(n1):
                    maxima(n1, m + 1, 0)
                if live(i - 1):
                    pe.wait_ge(yn_ready, i)

                    def free(k):
                        if live(n1):
                            pe.wait_ge(glo_ready2, 2 * n1 + k + 1)
                        else:
                            pe.wait_ge(out_ready2, 2 * (i - 3) + k + 1)

                    transposes(yn[:, n1s, :], yT_mm2, free)
                if live(n1):
                    maxima(n1, m + 1, 1)
                if live(i):
                    outputs(i, m, 2)
                if live(i - 1):
                    if live(n1):
                        pe.wait_ge(klo_ready, n1 + 1)
                    else:
                        pe.wait_ge(wlo_ready, i - 1)
                    if at(i, 1):
                        pe.wait_ge(r_ready, 1)
                    experts(i - 1, 0)
                if live(n1):
                    maxima(n1, m + 1, 2)
                    pe.wait_ge(klo_ready, n1 + 1)
                    if at(i, FIRST):
                        pe.wait_ge(wv_ready, 2)
                    for k in range(2):
                        if live(i - 1):
                            pe.wait_ge(yT1_ready if k else yT0_ready, i)
                        else:
                            pe.wait_ge(glo_ready2, 2 * n1 + k + 1)
                        half = slice(k * BANK, (k + 1) * BANK)
                        nc.tensor.matmul(T[:, k, :], k_hi[:, n1s, :], wv_st[:, half], start=True, stop=False)
                        nc.tensor.matmul(T[:, k, :], k_lo[:, n1s, :], wv_st[:, half], start=False,
                                         stop=True).then_inc(v_mm2, 1)
                if live(n1):
                    maxima(n1, m + 1, 3)
                if live(i - 1):
                    experts(i - 1, 1)

                def ffn(k):
                    if live(n1):
                        pe.wait_ge(vlo_ready2, 2 * n1 + k + 1)
                    elif live(i - 1):
                        pe.wait_ge(yT1_ready if k else yT0_ready, i)
                    else:
                        pe.wait_ge(out_ready2, 2 * (i - 3) + k + 1)
                    half = slice(k * BANK, (k + 1) * BANK)
                    nc.tensor.matmul(T[:, k, :], w_hi[:], b_hi[:, half], start=True, stop=False)
                    nc.tensor.matmul(T[:, k, :], w_hi[:], b_lo[:, half], start=False, stop=False)
                    nc.tensor.matmul(T[:, k, :], w_lo[:], b_hi[:, half], start=False, stop=True).then_inc(f_mm2, 1)

                if live(i - 2):
                    pe.wait_ge(wlo_ready, i - 1)
                    ffn(0)
                    ffn(1)
                if live(i):
                    outputs(i, m, 3)
                if live(n1):
                    pe.wait_ge(max_ready4, NG * n1 + NG)
                    if live(i - 1):
                        pe.wait_ge(h_ready, i)
                    else:
                        pe.wait_ge(klo_ready, n1 + 1)
                    nc.tensor.transpose(M[0:H, 0:P], nmax[:], ident[:]).then_inc(nT_mm, 1)
                if at(i, FIRST):
                    pe.wait_ge(a_in, 32)
                    pe.wait_ge(vlo_ready2, 2)
                    transposes(a_f, a_tr)
                    pe.wait_ge(nT_ready, 1)
                    for c in range(C):
                        last = nc.tensor.transpose(M[:, c * NX:(c + 1) * NX], r_f[:, c * P:(c + 1) * P],
                                                   ident[0:NX, 0:NX])
                    last.then_inc(r_tr, 1)
                    pe.wait_ge(b_in, 16 * C)
                    pe.wait_ge(a_ready, 2)
                    transposes(b_f[:].rearrange("p c e r -> p (c e r)"), b_tr)
                    pe.wait_ge(r_ready, 1)
                    pe.wait_ge(b_ready, 2)
                if live(n1):
                    scores(n1, m + 1, 0)

            pe.wait_ge(consts, 1 + 1 + NX + 2)
            pe.wait_ge(wq_in, 16)
            pe.wait_ge(wkv_ready, 2)
            pe.wait_ge(wqk_ready, 2)
            pipeline(pe, iteration)


_INS = ['x', 'ctx_4096', 'L0_xattn_Wq_d', 'L0_xattn_W_qk', 'L0_xattn_Wkv_d', 'L0_xattn_Wv_u',
        'L0_ffn_route_w', 'L0_ffn_A', 'L0_ffn_Bw']
_OUTS = [((16, 128, 1024), 'float32')]


def kernel(**inputs):
    import numpy as _np
    import concourse.bacc as _bacc
    from concourse import mybir as _mybir
    from concourse.bass_utils import run_bass_kernel_spmd as _run

    nc = _bacc.Bacc("TRN2", target_bir_lowering=False, num_devices=1)
    arrays, args = {}, []
    for name in _INS:
        a = _np.ascontiguousarray(inputs[name])
        arrays[f"in_{name}_dram"] = a
        args.append(nc.dram_tensor(f"in_{name}_dram", a.shape, _mybir.dt.from_np(a.dtype), kind="ExternalInput").ap())
    for i, (shape, dtype) in enumerate(_OUTS):
        dt = _mybir.dt.from_np(_np.dtype(dtype))
        args.append(nc.dram_tensor(f"out_{i}_dram", shape, dt, kind="ExternalOutput").ap())
    xattn_ffn_kernel(nc, *args)
    r = _run(nc, [arrays], core_ids=[0])
    return r.results[0]["out_0_dram"]
```

```python
import concourse.bass as bass
from concourse import mybir
from contextlib import ExitStack



def xattn_ffn_kernel(nc, x, ctx_in, w_q, w_qk, w_kv, w_v, route_w, a_w, b_w, out):
    f32, f16 = mybir.dt.float32, mybir.dt.float16
    ALU, ACT, AX = mybir.AluOpType, mybir.ActivationFunctionType, mybir.AxisListType

    NB, P, E = x.shape
    LQ = w_q.shape[1]
    L = w_kv.shape[1]
    H = w_qk.shape[1] // L
    HD = w_v.shape[1] // H
    NX, R, _ = a_w.shape
    ER = NX * R
    HR = ER + NX
    C = E // P
    HC = C // 2
    BANK = 512
    G4 = 4
    NG = H // G4
    OB = BANK // (HD + 1)
    OM = H - 2 * OB
    EPS = 1e-5
    WS = 16.0
    KS = 32.0
    BS = 64.0
    MS = 64.0
    SOFT = 1.0 / (WS * L ** 0.5)
    FS = 1.0 / (WS * BS)
    WARM = 36
    RING = 4
    FIRST, LAST, LOOP = -1, NB + 1, (4, NB - 4)

    with ExitStack() as stack:
        def sb(name, shape, dt):
            return stack.enter_context(nc.sbuf_tensor(name, shape, dt))

        def pb(name, shape):
            return stack.enter_context(nc.psum_tensor(name, shape, f32))

        def sem(name):
            return stack.enter_context(nc.semaphore(name))

        wq = sb("wq", [P, C, LQ], f32)
        wkv_f = sb("wkv_f", [P, C, L], f32)
        wkv_hi = sb("wkv_hi", [P, C, L], f16)
        wkv_lo = sb("wkv_lo", [P, C, L], f16)
        wqk_f = sb("wqk_f", [P, 2, C, L], f32)
        wqk_hi = sb("wqk_hi", [P, C, 2, L], f16)
        wqk_lo = sb("wqk_lo", [P, C, 2, L], f16)
        wv_f = sb("wv_f", [P, E], f32)
        wv_hi = sb("wv_hi", [P, E], f16)
        wv_st = sb("wv_st", [P, E], f16)
        a_f = sb("a_f", [P, E], f32)
        r_f = sb("r_f", [NX, E], f32)
        ar = sb("ar", [P, C, HR], f32)
        b_f = sb("b_f", [P, NX, C, R], f32)
        b_p = sb("b_p", [P, C, NX, R], f32)
        b_hi = sb("b_hi", [P, E], f16)
        b_lo = sb("b_lo", [P, E], f16)
        ident = sb("ident", [P, P], f32)
        pick = sb("pick", [H, H, P], f16)
        prefer = sb("prefer", [P, NX], f32)
        mhalf = sb("mhalf", [P, 1], f32)
        x_sb = sb("x_sb", [P, RING, E], f32)
        c_sb = sb("c_sb", [P, RING, E], f32)
        xn = sb("xn", [P, 2, E], f32)
        xT = sb("xT", [P, C, P], f32)
        c_hi = sb("c_hi", [P, C, P], f16)
        c_lo = sb("c_lo", [P, C, P], f16)
        k_f = sb("k_f", [P, 2, L], f32)
        q_hi = sb("q_hi", [P, P], f16)
        q_lo = sb("q_lo", [P, P], f16)
        k_hi = sb("k_hi", [P, 2, P], f16)
        k_lo = sb("k_lo", [P, 2, P], f16)
        g_hi = sb("g_hi", [P, 2, C, P], f16)
        g_lo = sb("g_lo", [P, 2, C, P], f16)
        v_hi = sb("v_hi", [P, 2, H, HD + 1], f16)
        v_lo = sb("v_lo", [P, 2, H, HD + 1], f16)
        nmax = sb("nmax", [P, H], f32)
        nmaxT = sb("nmaxT", [H, P], f16)
        prob = sb("prob", [P, NG, BANK], f32)
        p_hi = sb("p_hi", [P, NG, BANK], f16)
        p_lo = sb("p_lo", [P, NG, BANK], f16)
        rsum = sb("rsum", [P, H], f32)
        o_sb = sb("o_sb", [P, 2, E], f32)
        y_sb = sb("y_sb", [P, RING, E], f32)
        yn = sb("yn", [P, 2, E], f32)
        yT = sb("yT", [P, C, P], f32)
        h_sb = sb("h_sb", [P, HR], f32)
        top = sb("top", [P, 4], f32)
        tie = sb("tie", [P, NX], f32)
        rw = sb("rw", [P, NX], f32)
        wh = sb("wh", [P, NX, R], f32)
        w_hi = sb("w_hi", [P, P], f16)
        w_lo = sb("w_lo", [P, P], f16)
        o_out = sb("o_out", [P, 2, E], f32)
        bn = sb("bn", [P, 2, 2, 6], f32)
        mv = sb("mv", [P, 2, 2, 2], f32)
        ln = sb("ln", [P, 2, 3], f32)

        T = pb("T", [P, 2, BANK])
        S = pb("S", [P, BANK])
        D = pb("D", [P, 2, BANK])
        O = pb("O", [P, 2, BANK])
        M = pb("M", [P, BANK])

        x_in = [sem(f"x_in{n}") for n in range(RING)]
        c_in = [sem(f"c_in{n}") for n in range(RING)]
        wq_in, wkv_in, wqk_in, wv_in, a_in, b_in = (sem(n) for n in (
            "wq_in", "wkv_in", "wqk_in", "wv_in", "a_in", "b_in"))
        consts, apart = sem("consts"), sem("apart")
        wqk_ready, wvh_ready, wv_ready = sem("wqk_ready"), sem("wvh_ready"), sem("wv_ready")
        a_tr, a_ready, r_tr, r_ready = sem("a_tr"), sem("a_ready"), sem("r_tr"), sem("r_ready")
        b_scaled, b_tr, bhi_ready, b_ready = sem("b_scaled"), sem("b_tr"), sem("bhi_ready"), sem("b_ready")
        x_bn2, y_bn2, x_stat, y_stat = sem("x_bn2"), sem("y_bn2"), sem("x_stat"), sem("y_stat")
        x_ln, y_ln = sem("x_ln"), sem("y_ln")
        xn_ready, yn_ready, y_ready2 = sem("xn_ready"), sem("yn_ready"), sem("y_ready2")
        xT_mm2, xT_ready2 = sem("xT_mm2"), sem("xT_ready2")
        cT_mm2, chi_ready2, clo_ready2 = sem("cT_mm2"), sem("chi_ready2"), sem("clo_ready2")
        wkv_ready, k_mm, k_ready = sem("wkv_ready"), sem("k_mm"), sem("k_ready")
        yT_mm2, yT0_ready, yT1_ready = sem("yT_mm2"), sem("yT0_ready"), sem("yT1_ready")
        q_mm, qhi_ready, qlo_ready = sem("q_mm"), sem("qhi_ready"), sem("qlo_ready")
        kT_mm, khi_ready, klo_ready = sem("kT_mm"), sem("khi_ready"), sem("klo_ready")
        g_mm2, ghi_ready2, glo_ready2 = sem("g_mm2"), sem("ghi_ready2"), sem("glo_ready2")
        v_mm2, vhi_ready2, vlo_ready2 = sem("v_mm2"), sem("vhi_ready2"), sem("vlo_ready2")
        s_mm4, max_ready4 = sem("s_mm4"), sem("max_ready4")
        nT_mm, nT_ready = sem("nT_mm"), sem("nT_ready")
        d_mm4, phi_ready4, exp_ready4, plo_ready4 = sem("d_mm4"), sem("phi_ready4"), sem("exp_ready4"), sem("plo_ready4")
        pv_mm4, om_ready, o_ready = sem("pv_mm4"), sem("om_ready"), sem("o_ready")
        h_mm, h_ready, wh_ready = sem("h_mm"), sem("h_ready"), sem("wh_ready")
        wT_mm, whi_ready, wlo_ready = sem("wT_mm"), sem("whi_ready"), sem("wlo_ready")
        f_mm2, out_ready2 = sem("f_mm2"), sem("out_ready2")
        stored = [sem(f"stored{n}") for n in range(2)]
        o_step2, route4, pool_chain = sem("o_step2"), sem("route4"), sem("pool_chain")

        def live(b):
            return not isinstance(b, int) or 0 <= b < NB

        def at(i, n):
            return isinstance(i, int) and i == n

        def wait(eng, s, n):
            if not isinstance(n, int) or n > 0:
                eng.wait_ge(s, n)

        def wait_apart(eng, s, n):
            wait(eng, s, n)
            eng.sem_inc(apart, 1)

        def arrived(eng, s, b, m, ring):
            eng.wait_ge(s[m], (16 // ring) * (b - m) + 16)

        def in_chunks(bank):
            return bank.rearrange("p (c t) -> p c t", t=P)

        def b_chunks(b, k):
            return b[:].rearrange("p (t c) -> p c t", c=C)[:, k * HC:(k + 1) * HC, :]

        def pipeline(eng, iteration, first=FIRST, loop=LOOP, last=LAST):
            for i in range(first, loop[0]):
                iteration(i, i % RING)
            with eng.Fori(loop[0], loop[1] - RING + 1, RING) as i0:
                for n in range(RING):
                    iteration(i0 + n, (loop[0] + n) % RING)
            for i in range(loop[1], last + 1):
                iteration(i, i % RING)

        block = stack.enter_context(nc.Block())

        @block.sync
        def _(sp):
            def load(b, m):
                sp.dma_start(x_sb[:, m, :], x[b, :, :]).then_inc(x_in[m], 16)
                sp.dma_start(c_sb[:, m, :], ctx_in[b, :, :]).then_inc(c_in[m], 16)

            load(0, 0)
            sp.dma_start(wq[:], w_q.rearrange("(c p) n -> p c n", p=P)).then_inc(wq_in, 16)
            sp.dma_start(wkv_f[:], w_kv.rearrange("(c p) n -> p c n", p=P)).then_inc(wkv_in, 16)
            sp.dma_start(wqk_f[:], w_qk.rearrange("p (t c l) -> p t c l", t=2, l=L)).then_inc(wqk_in, 16)
            sp.dma_start(x_sb[:, 1, :], x[1, :, :]).then_inc(x_in[1], 16)
            for t in range(2):
                sp.dma_start(wv_f[t * L:(t + 1) * L, :], w_v).then_inc(wv_in, 16)
            sp.dma_start(c_sb[:, 1, :], ctx_in[1, :, :]).then_inc(c_in[1], 16)
            sp.dma_start(a_f[:], a_w.rearrange("e r d -> (e r) d")).then_inc(a_in, 16)
            sp.dma_start(r_f[:], route_w).then_inc(a_in, 16)
            sp.dma_start(b_f[:], b_w.rearrange("e (p c) r -> p e c r", p=P)).then_inc(b_in, 16)
            load(2, 2)

            def iteration(i, m):
                b = i + 3
                if live(b):
                    wait(sp, y_stat, i)
                    load(b, (m + 3) % RING)
                b = i - 2
                if at(i, LAST):
                    for k in range(2):
                        half = slice(k * BANK, (k + 1) * BANK)
                        sp.wait_ge(out_ready2, 2 * b + k + 1)
                        sp.dma_start(out[b, :, half], o_out[:, m % 2, half]).then_inc(stored[m % 2], 16)
                elif live(b):
                    sp.wait_ge(out_ready2, 2 * b + 2)
                    sp.dma_start(out[b, :, :], o_out[:, m % 2, :]).then_inc(stored[m % 2], 16)

            pipeline(sp, iteration, first=0, loop=(2, 10))
            for n in range(2):
                sp.wait_ge(stored[n], 16 * (NB // 2) + 16 * ((NB - 1) % 2 == n))

        @block.gpsimd
        def _(pool):
            chain = [0]

            def link(ins):
                chain[0] += 1
                ins.then_inc(pool_chain, 1)
                pool.wait_ge(pool_chain, chain[0])

            link(nc.gpsimd.memset(ident[:], 0.0))
            nc.gpsimd.affine_select(out=ident[:], in_=ident[:], compare_op=ALU.not_equal, fill=1.0, base=0,
                                    pattern=[[-1, P]], channel_multiplier=1).then_inc(consts, 1)
            link(nc.gpsimd.memset(mhalf[:], -0.5))
            link(nc.gpsimd.memset(pick[:], 0.0))
            nc.gpsimd.affine_select(out=pick[:], in_=pick[:], compare_op=ALU.not_equal, fill=MS, base=0,
                                    pattern=[[-1, H], [0, P]], channel_multiplier=1).then_inc(consts, 1)
            for e in range(NX):
                nc.gpsimd.memset(prefer[:, e:e + 1], float(NX - e)).then_inc(consts, 1)
            nc.gpsimd.memset(v_hi[:, :, :, HD:HD + 1], WS).then_inc(consts, 1)
            nc.gpsimd.memset(v_lo[:, :, :, HD:HD + 1], 0.0).then_inc(consts, 1)

            def normalise(dst, src, stat, which, b, ln_step, done):
                wait_apart(pool, done, b)
                part = ln[:, which, :]
                nc.gpsimd.tensor_scalar(part[:, 1:2], stat[:, 1:2], 1.0, EPS, ALU.mult, ALU.add).then_inc(ln_step, 1)
                nc.gpsimd.tensor_scalar(part[:, 0:1], stat[:, 0:1], -1.0, 0.0, ALU.mult, ALU.add).then_inc(ln_step, 1)
                wait_apart(pool, ln_step, 3 * b + 1)
                nc.gpsimd.tensor_tensor(part[:, 2:3], part[:, 1:2], mhalf[:], ALU.pow).then_inc(ln_step, 1)
                wait_apart(pool, ln_step, 3 * b + 3)
                nc.gpsimd.tensor_scalar(dst, src, part[:, 0:1], part[:, 2:3], ALU.add, ALU.mult).then_inc(done, 1)

            def iteration(i, m):
                def low(g):
                    pool.wait_ge(exp_ready4, NG * i + g + 1)
                    wait(pool, pv_mm4, NG * (i - 1) + g + 1)
                    nc.gpsimd.tensor_tensor(p_lo[:, g, :], prob[:, g, :], p_hi[:, g, :],
                                            ALU.subtract).then_inc(plo_ready4, 1)

                low_here = live(i) and not at(i, NB - 1)
                if low_here:
                    low(0)
                b = i - 1
                if live(b) and not at(i, NB):
                    pool.wait_ge(o_ready, b + 1)
                    wait(pool, out_ready2, 2 * (b - 2))
                    for k in range(2):
                        half = slice(k * BANK, (k + 1) * BANK)
                        nc.gpsimd.tensor_tensor(y_sb[:, (m - 1) % RING, half], x_sb[:, (m - 1) % RING, half],
                                                o_sb[:, (m - 1) % 2, half], ALU.add).then_inc(y_ready2, 1)
                if low_here:
                    low(1)
                if live(b):
                    pool.wait_ge(y_stat, b + 1)
                    wait(pool, yT_mm2, 2 * (b - 1))
                    normalise(yn[:, (m - 1) % 2, :], y_sb[:, (m - 1) % RING, :], mv[:, 1, (m - 1) % 2, :],
                              1, b, y_ln, yn_ready)
                if low_here:
                    low(2)
                b = i + 2
                if live(b):
                    pool.wait_ge(x_stat, b + 1)
                    wait(pool, xT_mm2, 2 * (b - 1))
                    normalise(xn[:, m % 2, :], x_sb[:, (m + 2) % RING, :], mv[:, 0, m % 2, :],
                              0, b, x_ln, xn_ready)
                if low_here:
                    low(3)
                if at(i, FIRST):
                    wait_apart(pool, b_in, 16)
                    nc.gpsimd.tensor_scalar(b_p[:].rearrange("p c e r -> p e c r"), b_f[:], BS, 0.0,
                                            ALU.mult, ALU.add).then_inc(b_scaled, 1)

            pipeline(pool, iteration, first=FIRST - 1)

        @block.vector
        def _(dve):
            def half_statistics(src, which, b, k, step, done):
                if k == 0:
                    wait(dve, done, b)
                nc.vector.bn_stats(bn[:, which, k, :], src[:, k * BANK:(k + 1) * BANK]).then_inc(step, 1)

            def statistics(which, b, slot, step, done):
                wait_apart(dve, step, 2 * b + 2)
                nc.vector.bn_aggr(mv[:, which, slot, :], bn[:, which, :, :]).then_inc(done, 1)

            def iteration(i, m):
                def maximum(g):
                    dve.wait_ge(s_mm4, NG * (i + 1) + g + 1)
                    h0 = C * (g % 2) + G4 * (g // 2)
                    nc.vector.tensor_reduce(nmax[:, h0:h0 + G4], S[:].rearrange("p (h t) -> p h t", t=P),
                                            AX.X, ALU.max, negate=True).then_inc(max_ready4, 1)

                def low(g):
                    dve.wait_ge(exp_ready4, NG * i + g + 1)
                    wait(dve, pv_mm4, NG * (i - 1) + g + 1)
                    nc.vector.tensor_tensor(p_lo[:, g, :], prob[:, g, :], p_hi[:, g, :],
                                            ALU.subtract).then_inc(plo_ready4, 1)

                def attention_output(b, n):
                    dve.wait_ge(pv_mm4, NG * b + NG)
                    wait(dve, y_ready2, 2 * (b - 1))
                    om = S[:, 0:OM * (HD + 1)].rearrange("p (h d) -> p h d", h=OM)
                    oe = O[:, :, 0:OB * (HD + 1)].rearrange("p k (h d) -> p k h d", h=OB)
                    slot = o_sb[:, n % 2, :]
                    nc.vector.reciprocal(rsum[:, 2 * OB:H], om[:, :, HD]).then_inc(o_step2, 1)
                    re = rsum[:, 0:2 * OB].rearrange("p (k h) -> p k h", k=2)
                    nc.vector.reciprocal(re, oe[:, :, :, HD]).then_inc(o_step2, 1)
                    dve.wait_ge(o_step2, 2 * b + 2)
                    nc.vector.tensor_tensor(
                        slot[:, 2 * OB * HD:E].rearrange("p (h d) -> p h d", h=OM), om[:, :, 0:HD],
                        rsum[:, 2 * OB:H].unsqueeze(2).broadcast_to([P, OM, HD]), ALU.mult).then_inc(om_ready, 1)
                    nc.vector.tensor_tensor(
                        slot[:, 0:2 * OB * HD].rearrange("p (k h d) -> p k h d", k=2, h=OB), oe[:, :, :, 0:HD],
                        re.unsqueeze(3).broadcast_to([P, 2, OB, HD]), ALU.mult).then_inc(o_ready, 1)

                def y_half(b, n, k):
                    dve.wait_ge(y_ready2, 2 * b + k + 1)
                    half_statistics(y_sb[:, n % RING, :], 1, b, k, y_bn2, y_stat)

                def y_both(b, n):
                    wait(dve, yn_ready, b - 1)
                    statistics(1, b, n % 2, y_bn2, y_stat)

                if live(i - 1) and not at(i, NB):
                    attention_output(i - 1, m - 1)
                if at(i, NB - 1):
                    low(0)
                    low(1)
                b = i - 2
                if live(b):
                    dve.wait_ge(whi_ready, b + 1)
                    wait(dve, f_mm2, 2 * b)
                    nc.vector.scalar_tensor_tensor(w_lo[:], M[:, 0:P], WS, w_hi[:], ALU.mult,
                                                   ALU.subtract).then_inc(wlo_ready, 1)
                if at(i, FIRST):
                    dve.wait_ge(consts, 1 + 1 + NX + 2)
                    dve.wait_ge(wkv_in, 16)
                    dve.wait_ge(wkv_ready, 1)
                    nc.vector.scalar_tensor_tensor(wkv_lo[:], wkv_f[:], KS, wkv_hi[:],
                                                   ALU.mult, ALU.subtract).then_inc(wkv_ready, 1)

                def x_statistics(b):
                    arrived(dve, x_in, b, (m + 2) % RING, RING)
                    wait(dve, xn_ready, b - 1)
                    for k in range(2):
                        half_statistics(x_sb[:, (m + 2) % RING, :], 0, b, k, x_bn2, x_stat)
                    statistics(0, b, m % 2, x_bn2, x_stat)

                if live(i - 1) and not at(i, NB):
                    y_half(i - 1, m - 1, 0)
                if at(i, NB - 1):
                    low(2)
                b, s = i + 1, (m + 1) % 2
                if live(b):
                    wait(dve, k_mm, b)
                    for k in range(2):
                        dve.wait_ge(chi_ready2, 2 * b + k + 1)
                        nc.vector.tensor_tensor(c_lo[:, k * HC:(k + 1) * HC, :], T[:, k, :].rearrange(
                            "p (j t) -> p j t", t=P), c_hi[:, k * HC:(k + 1) * HC, :],
                            ALU.subtract).then_inc(clo_ready2, 1)
                    dve.wait_ge(qhi_ready, b + 1)
                    wait(dve, g_mm2, 2 * b)
                    nc.vector.tensor_tensor(q_lo[:], M[:, 0:P], q_hi[:], ALU.subtract).then_inc(qlo_ready, 1)
                if at(i, FIRST):
                    dve.wait_ge(wqk_in, 16)
                    dve.wait_ge(wqk_ready, 2)
                    for t in range(2):
                        nc.vector.scalar_tensor_tensor(wqk_lo[:, :, t, :], wqk_f[:, t, :, :], WS, wqk_hi[:, :, t, :],
                                                       ALU.mult, ALU.subtract).then_inc(wqk_ready, 1)
                    x_statistics(i + 2)
                if live(i - 1) and not at(i, NB):
                    y_half(i - 1, m - 1, 1)
                    y_both(i - 1, m - 1)
                if live(i + 2) and not at(i, FIRST):
                    x_statistics(i + 2)
                if at(i, NB - 1):
                    low(3)
                    attention_output(i, m)
                    dve.wait_ge(o_ready, i + 1)
                    for k in range(2):
                        half = slice(k * BANK, (k + 1) * BANK)
                        nc.vector.tensor_tensor(y_sb[:, m, half], x_sb[:, m, half], o_sb[:, m % 2, half],
                                                ALU.add).then_inc(y_ready2, 1)
                b = i + 1
                if live(b):
                    wait(dve, d_mm4, NG * (b - 1))
                    for k in range(2):
                        dve.wait_ge(ghi_ready2, 2 * b + k + 1)
                        nc.vector.tensor_tensor(g_lo[:, s, k * HC:(k + 1) * HC, :], T[:, k, :].rearrange(
                            "p (j t) -> p j t", t=P), g_hi[:, s, k * HC:(k + 1) * HC, :],
                            ALU.subtract).then_inc(glo_ready2, 1)
                    dve.wait_ge(khi_ready, b + 1)
                    nc.vector.tensor_tensor(k_lo[:, s, :], M[:, 0:P], k_hi[:, s, :],
                                            ALU.subtract).then_inc(klo_ready, 1)
                if at(i, NB - 1):
                    y_half(i, m, 0)
                    y_half(i, m, 1)
                    y_both(i, m)
                if live(i + 1):
                    wait(dve, nT_mm, i + 1)
                    maximum(0)
                if at(i, FIRST):
                    dve.wait_ge(wv_in, 32)
                    dve.wait_ge(wvh_ready, 1)
                    nc.vector.scalar_tensor_tensor(wv_st[L:P, :], wv_f[L:P, :], WS, wv_hi[L:P, :],
                                                   ALU.mult, ALU.subtract).then_inc(wv_ready, 1)
                b = i - 1
                if live(b) and not at(i, NB - 1):
                    dve.wait_ge(yT_mm2, 2 * b + 2)
                    wait(dve, h_mm, b)
                    nc.vector.tensor_copy(yT[:, HC:C, :], T[:, 1, :].rearrange(
                        "p (j t) -> p j t", t=P)).then_inc(yT1_ready, 1)
                b = i + 1
                if live(b):
                    maximum(1)
                    maximum(2)
                    if not live(i - 1):
                        maximum(3)
                    wait(dve, pv_mm4, NG * (b - 1))
                    for k in range(2):
                        dve.wait_ge(vhi_ready2, 2 * b + k + 1)
                        hs = slice(k * (H // 2), (k + 1) * (H // 2))
                        nc.vector.tensor_tensor(v_lo[:, s, hs, 0:HD], T[:, k, :].rearrange(
                            "p (h d) -> p h d", d=HD), v_hi[:, s, hs, 0:HD], ALU.subtract).then_inc(vlo_ready2, 1)
                    if live(i - 1):
                        maximum(3)
                b = i - 1
                if live(b):
                    dve.wait_ge(h_ready, b + 1)
                    wait(dve, wT_mm, b)
                    logits = h_sb[:, ER:HR]
                    nc.vector.tensor_reduce(top[:, 0:1], logits, AX.X, ALU.max).then_inc(route4, 1)
                    dve.wait_ge(route4, 4 * b + 1)
                    nc.vector.scalar_tensor_tensor(tie[:], logits, top[:, 0:1], prefer[:], ALU.is_equal,
                                                   ALU.mult).then_inc(route4, 1)
                    dve.wait_ge(route4, 4 * b + 2)
                    nc.vector.tensor_reduce(top[:, 1:2], tie[:], AX.X, ALU.max).then_inc(route4, 1)
                    dve.wait_ge(route4, 4 * b + 3)
                    nc.vector.tensor_scalar(rw[:], tie[:], top[:, 1:2], top[:, 0:1], ALU.is_equal,
                                            ALU.mult).then_inc(route4, 1)
                    dve.wait_ge(route4, 4 * b + 4)
                    nc.vector.tensor_tensor(wh[:], h_sb[:, 0:ER].rearrange("p (e r) -> p e r", e=NX),
                                            rw[:].unsqueeze(2).broadcast_to([P, NX, R]),
                                            ALU.mult).then_inc(wh_ready, 1)
                b = i - 2
                if live(b):
                    wait(dve, stored[m % 2], 8 * (b - m % 2))
                    for k in range(2):
                        dve.wait_ge(f_mm2, 2 * b + k + 1)
                        half = slice(k * BANK, (k + 1) * BANK)
                        nc.vector.scalar_tensor_tensor(o_out[:, m % 2, half], T[:, k, :], FS,
                                                       y_sb[:, (m - 2) % RING, half], ALU.mult,
                                                       ALU.add).then_inc(out_ready2, 1)
                if at(i, FIRST):
                    for k in range(2):
                        dve.wait_ge(bhi_ready, k + 1)
                        nc.vector.tensor_tensor(b_chunks(b_lo, k), in_chunks(O[:, k, :]), b_chunks(b_hi, k),
                                                ALU.subtract).then_inc(b_ready, 1)

            pipeline(dve, iteration, first=FIRST - 1)

        @block.scalar
        def _(act):
            def copy_out(dst, mm, free, free_n, done, b):
                wait(act, free, free_n)
                for k in range(2):
                    act.wait_ge(mm, 2 * b + k + 1)
                    nc.scalar.activation(dst[:, k * HC:(k + 1) * HC, :], T[:, k, :].rearrange(
                        "p (j t) -> p j t", t=P), ACT.Copy).then_inc(done, 1)

            def exps(b, g, between=None):
                act.wait_ge(d_mm4, NG * b + g + 1)
                wait(act, pv_mm4, NG * (b - 1) + g + 1)
                nc.scalar.activation(p_hi[:, g, :], D[:, g % 2, :], ACT.Exp, scale=SOFT).then_inc(phi_ready4, 1)
                if between:
                    between()
                nc.scalar.activation(prob[:, g, :], D[:, g % 2, :], ACT.Exp, scale=SOFT).then_inc(exp_ready4, 1)

            def iteration(i, m):
                s = (m + 1) % 2
                b = i - 2
                if live(b):
                    act.wait_ge(wT_mm, b + 1)
                    wait(act, f_mm2, 2 * b)
                    nc.scalar.activation(w_hi[:], M[:, 0:P], ACT.Copy, scale=WS).then_inc(whi_ready, 1)
                if live(i + 1):
                    copy_out(xT, xT_mm2, q_mm, i + 1, xT_ready2, i + 1)
                if at(i, FIRST):
                    act.wait_ge(wkv_in, 16)
                    nc.scalar.activation(wkv_hi[:], wkv_f[:], ACT.Copy, scale=KS).then_inc(wkv_ready, 1)
                if live(i):
                    exps(i, 1)
                b = i + 1
                if live(b):
                    copy_out(c_hi, cT_mm2, k_mm, b, chi_ready2, b)
                    if at(i, FIRST):
                        act.wait_ge(wqk_in, 16)
                        for t in range(2):
                            nc.scalar.activation(wqk_hi[:, :, t, :], wqk_f[:, t, :, :], ACT.Copy,
                                                 scale=WS).then_inc(wqk_ready, 1)
                    act.wait_ge(q_mm, b + 1)
                    wait(act, g_mm2, 2 * b)
                    nc.scalar.activation(q_hi[:], M[:, 0:P], ACT.Copy).then_inc(qhi_ready, 1)
                if live(i):
                    exps(i, 2)
                if live(b):
                    act.wait_ge(k_mm, b + 1)
                    wait(act, kT_mm, b)
                    nc.scalar.activation(k_f[:], M[:, 0:L].unsqueeze(1).broadcast_to([P, 2, L]), ACT.Copy,
                                         scale=1.0 / KS).then_inc(k_ready, 1)
                    wait(act, d_mm4, NG * (b - 1))
                    wait(act, v_mm2, 2 * (b - 1))
                    for k in range(2):
                        act.wait_ge(g_mm2, 2 * b + k + 1)
                        nc.scalar.activation(g_hi[:, s, k * HC:(k + 1) * HC, :], T[:, k, :].rearrange(
                            "p (j t) -> p j t", t=P), ACT.Copy).then_inc(ghi_ready2, 1)
                    act.wait_ge(kT_mm, b + 1)
                    nc.scalar.activation(k_hi[:, s, :], M[:, 0:P], ACT.Copy).then_inc(khi_ready, 1)
                if at(i, FIRST):
                    act.wait_ge(wv_in, 32)
                    nc.scalar.activation(wv_hi[L:P, :], wv_f[L:P, :], ACT.Copy, scale=WS).then_inc(wvh_ready, 1)
                    nc.scalar.activation(wv_st[0:L, :], wv_f[0:L, :], ACT.Copy, scale=WS).then_inc(wv_ready, 1)
                    for k in range(2):
                        act.wait_ge(a_tr, k + 1)
                        nc.scalar.activation(ar[:, k * HC:(k + 1) * HC, 0:ER], in_chunks(D[:, k, :]),
                                             ACT.Copy).then_inc(a_ready, 1)

                def copy_yT0():
                    act.wait_ge(yT_mm2, 2 * i - 1)
                    wait(act, h_mm, i - 1)
                    nc.scalar.activation(yT[:, 0:HC, :], T[:, 0, :].rearrange(
                        "p (j t) -> p j t", t=P), ACT.Copy).then_inc(yT0_ready, 1)

                if live(i):
                    exps(i, 3, copy_yT0 if live(i - 1) and not at(i, NB - 1) else None)
                if at(i, NB - 1) or at(i, NB):
                    copy_yT0()
                if at(i, NB - 1):
                    act.wait_ge(yT_mm2, 2 * i)
                    nc.scalar.activation(yT[:, HC:C, :], in_chunks(T[:, 1, :]), ACT.Copy).then_inc(yT1_ready, 1)
                if live(b):
                    wait(act, pv_mm4, NG * (b - 1))
                    for k in range(2):
                        act.wait_ge(v_mm2, 2 * b + k + 1)
                        nc.scalar.activation(v_hi[:, s, k * (H // 2):(k + 1) * (H // 2), 0:HD], T[:, k, :].rearrange(
                            "p (h d) -> p h d", d=HD), ACT.Copy).then_inc(vhi_ready2, 1)
                if live(i - 1):
                    act.wait_ge(h_mm, i)
                    wait(act, wh_ready, i - 1)
                    nc.scalar.activation(h_sb[:], M[:, 0:HR], ACT.Copy).then_inc(h_ready, 1)
                if at(i, FIRST):
                    act.wait_ge(r_tr, 1)
                    nc.scalar.activation(ar[:, :, ER:HR], O[:, 0, 0:C * NX].rearrange("p (c e) -> p c e", e=NX),
                                         ACT.Copy).then_inc(r_ready, 1)
                    for k in range(2):
                        act.wait_ge(b_tr, k + 1)
                        nc.scalar.activation(b_chunks(b_hi, k), in_chunks(O[:, k, :]),
                                             ACT.Copy).then_inc(bhi_ready, 1)
                if live(b):
                    act.wait_ge(nT_mm, b + 1)
                    wait(act, d_mm4, NG * b)
                    nc.scalar.activation(nmaxT[:], M[0:H, 0:P], ACT.Copy, scale=1.0 / MS).then_inc(nT_ready, 1)
                if live(b):
                    exps(b, 0)

            pipeline(act, iteration)

        @block.tensor
        def _(pe):
            def transposes(chunk, mm, free=None, banks=T):
                for c in range(C):
                    if c % HC == 0 and free:
                        free(c // HC)
                    last = nc.tensor.transpose(banks[:, c // HC, (c % HC) * P:(c % HC + 1) * P], chunk(c), ident[:])
                    if c % HC == HC - 1:
                        last.then_inc(mm, 1)

            def chunks_of(src):
                return lambda c: src[:, c * P:(c + 1) * P]

            def scores(b, m, g):
                if at(b, 0) and g == 0:
                    pe.wait_ge(a_ready, 2)
                if g == 0:
                    pe.wait_ge(klo_ready, b + 1)
                    pe.wait_ge(glo_ready2, 2 * b + 2)
                wait(pe, exp_ready4, NG * b + g - 1)
                s, j0 = m % 2, G4 * (g // 2)
                rows = slice(L * (g % 2), L * (g % 2 + 1))
                d = D[:, g % 2, :]
                hi = g_hi[rows, s, j0:j0 + G4, :].rearrange("p j t -> p (j t)")
                lo = g_lo[rows, s, j0:j0 + G4, :].rearrange("p j t -> p (j t)")
                nc.tensor.matmul(d, k_hi[rows, s, :], hi, start=True, stop=False)
                nc.tensor.matmul(d, k_hi[rows, s, :], lo, start=False, stop=False)
                nc.tensor.matmul(d, k_lo[rows, s, :], hi, start=False, stop=False)
                if g == 0:
                    pe.wait_ge(nT_ready, b + 1)
                for n in range(G4):
                    last = nc.tensor.matmul(d[:, n * P:(n + 1) * P], pick[:, C * (g % 2) + j0 + n, :], nmaxT[:],
                                            start=False, stop=(n == G4 - 1))
                last.then_inc(d_mm4, 1)

            def outputs(b, m, g):
                if at(b, 0) and g == 0:
                    pe.wait_ge(b_ready, 2)
                if g == 0:
                    pe.wait_ge(vlo_ready2, 2 * b + 2)
                    wait(pe, o_ready, b)
                if g == NG - 1 and live(b + 1):
                    pe.wait_ge(max_ready4, NG * (b + 1) + NG)
                pe.wait_ge(plo_ready4, NG * b + g + 1)
                for n in range(G4):
                    h = C * (g % 2) + G4 * (g // 2) + n
                    bank = S if h >= 2 * OB else O[:, h // OB, :]
                    col = (h % OB) * (HD + 1)
                    o = bank[:, col:col + HD + 1]
                    hi, lo = p_hi[:, g, n * P:(n + 1) * P], p_lo[:, g, n * P:(n + 1) * P]
                    nc.tensor.matmul(o, hi, v_hi[:, m % 2, h, :], start=True, stop=False)
                    nc.tensor.matmul(o, hi, v_lo[:, m % 2, h, :], start=False, stop=False)
                    last = nc.tensor.matmul(o, lo, v_hi[:, m % 2, h, :], start=False, stop=True)
                last.then_inc(pv_mm4, 1)

            def maxima(b, m, g):
                if g == 0:
                    pe.wait_ge(khi_ready, b + 1)
                    pe.wait_ge(ghi_ready2, 2 * b + 2)
                wait(pe, max_ready4, NG * b + g)
                if g == 0:
                    wait(pe, om_ready, b - 1)
                rows = slice(L * (g % 2), L * (g % 2 + 1))
                for n in range(G4):
                    last = nc.tensor.matmul(S[:, n * P:(n + 1) * P], g_hi[rows, m % 2, G4 * (g // 2) + n, :],
                                            k_hi[rows, m % 2, :], start=True, stop=True)
                last.then_inc(s_mm4, 1)

            def experts(b, k):
                pe.wait_ge(yT1_ready if k else yT0_ready, b + 1)
                for c in range(k * HC, (k + 1) * HC):
                    last = nc.tensor.matmul(M[:, 0:HR], yT[:, c, :], ar[:, c, :], start=(c == 0), stop=(c == C - 1))
                if k == 1:
                    last.then_inc(h_mm, 1)

            def iteration(i, m):
                n1, n1s = i + 1, (m + 1) % 2
                b = i - 2
                if live(b):
                    pe.wait_ge(wh_ready, b + 1)
                    if live(i):
                        pe.wait_ge(nT_ready, i + 1)
                    else:
                        wait(pe, h_ready, min(i - 1, NB))
                    nc.tensor.transpose(M[:, 0:P], wh[:].rearrange("p e r -> p (e r)"), ident[:]).then_inc(wT_mm, 1)
                if live(n1):
                    pe.wait_ge(xn_ready, n1 + 1)

                    def free(k):
                        wait(pe, vlo_ready2, 2 * i + k + 1)
                        if not isinstance(i, int) or i >= 3:
                            pe.wait_ge(out_ready2, 2 * (i - 3) + k + 1)

                    transposes(chunks_of(xn[:, n1s, :]), xT_mm2, None if at(i, FIRST) else free)
                if live(i):
                    scores(i, m, 1)
                if live(n1):
                    arrived(pe, c_in, n1, (m + 1) % RING, RING)
                    transposes(chunks_of(c_sb[:, (m + 1) % RING, :]), cT_mm2,
                               lambda k: pe.wait_ge(xT_ready2, 2 * n1 + k + 1))
                    if live(i - 2):
                        pe.wait_ge(wlo_ready, i - 1)
                    else:
                        wait(pe, nT_ready, n1)
                    if at(i, FIRST):
                        pe.wait_ge(wq_in, 16)
                    for c in range(C):
                        last = nc.tensor.matmul(M[:, 0:P], wq[:, c, :], xT[:, c, :], start=(c == 0), stop=(c == C - 1))
                    last.then_inc(q_mm, 1)
                if at(i, NB - 1):
                    scores(i, m, 2)
                    scores(i, m, 3)
                    outputs(i, m, 0)
                elif live(i):
                    outputs(i, m, 0)
                    scores(i, m, 2)
                if live(n1):
                    pe.wait_ge(clo_ready2, 2 * n1 + 2)
                    if at(i, FIRST):
                        pe.wait_ge(wkv_ready, 2)
                    pe.wait_ge(qlo_ready, n1 + 1)
                    for c in range(C):
                        k = M[:, 0:L]
                        nc.tensor.matmul(k, c_hi[:, c, :], wkv_hi[:, c, :], start=(c == 0), stop=False)
                        nc.tensor.matmul(k, c_hi[:, c, :], wkv_lo[:, c, :], start=False, stop=False)
                        last = nc.tensor.matmul(k, c_lo[:, c, :], wkv_hi[:, c, :], start=False, stop=(c == C - 1))
                    last.then_inc(k_mm, 1)
                    if at(i, FIRST):
                        pe.wait_ge(wqk_ready, 4)
                    for j in range(C):
                        g = T[:, j // HC, (j % HC) * P:(j % HC + 1) * P]
                        w = [part[:, j, :, :].rearrange("p t l -> p (t l)") for part in (wqk_hi, wqk_lo)]
                        nc.tensor.matmul(g, w[0], q_hi[:], start=True, stop=False)
                        nc.tensor.matmul(g, w[0], q_lo[:], start=False, stop=False)
                        last = nc.tensor.matmul(g, w[1], q_hi[:], start=False, stop=True)
                        if j % HC == HC - 1:
                            last.then_inc(g_mm2, 1)
                    pe.wait_ge(k_ready, n1 + 1)
                    nc.tensor.transpose(M[:, 0:P], k_f[:].rearrange("p t l -> p (t l)"), ident[:]).then_inc(kT_mm, 1)
                if live(i):
                    outputs(i, m, 1)
                    if live(i - 1) and not at(i, NB - 1):
                        scores(i, m, 3)
                if live(n1):
                    maxima(n1, m + 1, 0)
                if at(i, 0):
                    scores(i, m, 3)
                if at(i, FIRST):
                    pe.wait_ge(a_in, 32)
                    transposes(chunks_of(a_f), a_tr, banks=D)
                if at(i, NB - 1):
                    outputs(i, m, 2)
                    outputs(i, m, 3)
                if live(i - 1):
                    pe.wait_ge(yn_ready, i)

                    def free(k):
                        if live(n1):
                            pe.wait_ge(glo_ready2, 2 * n1 + k + 1)
                        else:
                            pe.wait_ge(out_ready2, 2 * (i - 3) + k + 1)

                    transposes(chunks_of(yn[:, n1s, :]), yT_mm2, free)
                if live(n1):
                    maxima(n1, m + 1, 1)
                if at(i, FIRST):
                    for c in range(C):
                        last = nc.tensor.transpose(O[:, 0, c * NX:(c + 1) * NX], r_f[:, c * P:(c + 1) * P],
                                                   ident[0:NX, 0:NX])
                    last.then_inc(r_tr, 1)
                if live(i) and not at(i, NB - 1) and not at(i, 0):
                    outputs(i, m, 2)
                if live(n1):
                    pe.wait_ge(klo_ready, n1 + 1)
                    if at(i, FIRST):
                        pe.wait_ge(wv_ready, 2)
                    for k in range(2):
                        if live(i - 1):
                            pe.wait_ge(yT1_ready if k else yT0_ready, i)
                        else:
                            pe.wait_ge(glo_ready2, 2 * n1 + k + 1)
                        half = slice(k * BANK, (k + 1) * BANK)
                        nc.tensor.matmul(T[:, k, :], k_hi[:, n1s, :], wv_st[:, half], start=True, stop=False)
                        nc.tensor.matmul(T[:, k, :], k_lo[:, n1s, :], wv_st[:, half], start=False,
                                         stop=True).then_inc(v_mm2, 1)
                if live(n1):
                    maxima(n1, m + 1, 2)
                if live(i - 1):
                    if live(n1):
                        pe.wait_ge(klo_ready, n1 + 1)
                    else:
                        pe.wait_ge(wlo_ready, i - 1)
                    if at(i, 1):
                        pe.wait_ge(r_ready, 1)
                    experts(i - 1, 0)
                if at(i, 0):
                    outputs(i, m, 2)
                if live(n1):
                    maxima(n1, m + 1, 3)
                if at(i, FIRST):
                    pe.wait_ge(b_scaled, 1)
                    pe.wait_ge(r_ready, 1)
                    transposes(lambda c: b_p[:, c, :, :].rearrange("p e r -> p (e r)"), b_tr, banks=O)
                if live(i - 1):
                    experts(i - 1, 1)

                def ffn(k):
                    if live(n1):
                        pe.wait_ge(vlo_ready2, 2 * n1 + k + 1)
                    elif live(i - 1):
                        pe.wait_ge(yT1_ready if k else yT0_ready, i)
                    else:
                        pe.wait_ge(out_ready2, 2 * (i - 3) + k + 1)
                    half = slice(k * BANK, (k + 1) * BANK)
                    nc.tensor.matmul(T[:, k, :], w_hi[:], b_hi[:, half], start=True, stop=False)
                    nc.tensor.matmul(T[:, k, :], w_hi[:], b_lo[:, half], start=False, stop=False)
                    if k == 0:
                        pe.wait_ge(wlo_ready, i - 1)
                    nc.tensor.matmul(T[:, k, :], w_lo[:], b_hi[:, half], start=False, stop=True).then_inc(f_mm2, 1)

                if live(i - 2):
                    pe.wait_ge(whi_ready, i - 1)
                    ffn(0)
                    ffn(1)
                if live(i) and not at(i, NB - 1):
                    outputs(i, m, 3)
                if live(n1):
                    pe.wait_ge(max_ready4, NG * n1 + NG)
                    if live(i - 1):
                        pe.wait_ge(h_ready, i)
                    else:
                        pe.wait_ge(klo_ready, n1 + 1)
                    nc.tensor.transpose(M[0:H, 0:P], nmax[:], ident[:]).then_inc(nT_mm, 1)
                if live(n1):
                    scores(n1, m + 1, 0)

            pe.wait_ge(consts, 1)
            for n in range(WARM):
                nc.tensor.transpose(O[:, 0, 0:P], ident[:], ident[:])
            pe.wait_ge(consts, 1 + 1 + NX + 2)
            pipeline(pe, iteration)


_INS = ['x', 'ctx_4096', 'L0_xattn_Wq_d', 'L0_xattn_W_qk', 'L0_xattn_Wkv_d', 'L0_xattn_Wv_u',
        'L0_ffn_route_w', 'L0_ffn_A', 'L0_ffn_Bw']
_OUTS = [((16, 128, 1024), 'float32')]


def kernel(**inputs):
    import numpy as _np
    import concourse.bacc as _bacc
    from concourse import mybir as _mybir
    from concourse.bass_utils import run_bass_kernel_spmd as _run

    nc = _bacc.Bacc("TRN2", target_bir_lowering=False, num_devices=1)
    arrays, args = {}, []
    for name in _INS:
        a = _np.ascontiguousarray(inputs[name])
        arrays[f"in_{name}_dram"] = a
        args.append(nc.dram_tensor(f"in_{name}_dram", a.shape, _mybir.dt.from_np(a.dtype), kind="ExternalInput").ap())
    for i, (shape, dtype) in enumerate(_OUTS):
        dt = _mybir.dt.from_np(_np.dtype(dtype))
        args.append(nc.dram_tensor(f"out_{i}_dram", shape, dt, kind="ExternalOutput").ap())
    xattn_ffn_kernel(nc, *args)
    r = _run(nc, [arrays], core_ids=[0])
    return r.results[0]["out_0_dram"]
```
